# Optimizing a Trainium2 kernel written in Bass

```python
import numpy as np
import jax
import jax.numpy as jnp

def _softmax(x, axis=-1):
    return jax.nn.softmax(x, axis=axis)

def _gelu(x):
    return jax.nn.gelu(x, approximate=True)

def _silu(x):
    return jax.nn.silu(x)

def _sigmoid(x):
    return jax.nn.sigmoid(x)

def _layernorm(x, axis=-1, eps=1e-05):
    m = jnp.mean(x, axis=axis, keepdims=True)
    v = jnp.var(x, axis=axis, keepdims=True)
    return (x - m) / jnp.sqrt(v + eps)

def _scatter_add(tgt, idx, src, axis=0):
    return tgt.at[idx].add(src)

def _segment_sum(src, seg, n):
    return jax.ops.segment_sum(src, seg, n)
kernel_name = 'mk_decoder_postln_d1_seqx_r4_746a5a'

def setup_inputs(seed: int=0):
    np.random.seed(seed)
    _w = jnp.asarray

    def _rec_inputs():
        import jax
        import jax.numpy as jnp
        _rk = jax.random.key(seed)
        x = 7.22e-05 + 1 * jax.random.normal(jax.random.fold_in(_rk, 1), (16, 512, 256), jnp.float32)
        _lenS = 512 - jax.random.randint(jax.random.fold_in(_rk, 7), (16,), 0, max(1, 512 // 4) + 1, jnp.int32)
        _lenS2 = 64 - jax.random.randint(jax.random.fold_in(_rk, 8), (16,), 0, max(1, 64 // 4) + 1, jnp.int32)
        _ctx_1024P = jax.random.normal(jax.random.fold_in(_rk, 11), (16, 16, 256), jnp.float32)
        _ctx_1024c = jax.random.dirichlet(jax.random.fold_in(_rk, 511), 0.3 * jnp.ones((16,), jnp.float32), (16, 64))
        _ctx_1024t = jnp.einsum('bsk,bkd->bsd', _ctx_1024c, _ctx_1024P)
        _ctx_1024t = _ctx_1024t * jax.lax.rsqrt(jnp.mean(jnp.square(_ctx_1024t)) + 1e-12) * 0.953939
        ctx_1024 = -1.39393e-06 + 0.999914 * (_ctx_1024t + 0.3 * jax.random.normal(jax.random.fold_in(_rk, 611), (16, 64, 256), jnp.float32))
        _validS = jnp.arange(512)[None, :] < _lenS[:, None]
        _validS2 = jnp.arange(64)[None, :] < _lenS2[:, None]
        _causal = jnp.tril(jnp.ones((512, 512), dtype=bool))
        mask_BxS2_bf1 = jnp.ones((16, 64), dtype=bool)
        return (x, ctx_1024, mask_BxS2_bf1)
    x, ctx_1024, mask_BxS2_bf1 = _rec_inputs()

    def _L0_attn_setup():
        import jax, jax.numpy as jnp
        import numpy as np
        C = 256
        H = 16
        K = 2
        B, N = (4, 1024)

        def _heads(t):
            shp = t.shape
            d = shp[-1] // H
            t = t.reshape(shp[:-1] + (H, d))
            return jnp.swapaxes(t, -2, -3)
        key = jax.random.key(seed)
        ks_ = jax.random.split(key, 12)
        s = 1.0 / np.sqrt(C)
        inp = {'x': jax.random.normal(ks_[0], (B, N, C), dtype=jnp.float32), 'Wq': jax.random.normal(ks_[1], (C, C), dtype=jnp.float32) * s, 'bq': jnp.zeros((C,), dtype=jnp.float32), 'Wk': jax.random.normal(ks_[2], (K, C, C), dtype=jnp.float32) * s, 'bk': jnp.zeros((K, C), dtype=jnp.float32), 'Wv': jax.random.normal(ks_[3], (K, C, C), dtype=jnp.float32) * s, 'bv': jnp.zeros((K, C), dtype=jnp.float32), 'Wo': jax.random.normal(ks_[4], (C, C), dtype=jnp.float32) * s, 'bo': jnp.zeros((C,), dtype=jnp.float32), 'ln_g': jnp.ones((C,), dtype=jnp.float32), 'ln_b': jnp.zeros((C,), dtype=jnp.float32)}
        return inp
    _L0_attn_all = _L0_attn_setup()
    _L0_attn_in = {k: v for k, v in _L0_attn_all.items() if k in ('Wq', 'bq', 'Wk', 'bk', 'Wv', 'bv', 'Wo', 'bo', 'ln_g', 'ln_b')}
    del _L0_attn_all

    def _L0_xattn_setup():
        import jax, jax.numpy as jnp
        import numpy as np
        HEADS = 16
        DIM_HEAD = 64
        SCALE = DIM_HEAD ** (-0.5)
        key = jax.random.key(seed)
        ks = jax.random.split(key, 6)
        B, Nq, Nkv, D = (4, 512, 256, 256)
        inner = HEADS * DIM_HEAD
        return {'x': jax.random.normal(ks[0], (B, Nq, D), dtype=jnp.float32), 'context': jax.random.normal(ks[1], (B, Nkv, D), dtype=jnp.float32), 'mask': jnp.ones((B, Nkv), dtype=bool), 'Wq': jax.random.normal(ks[2], (inner, D), dtype=jnp.float32) * D ** (-0.5), 'Wkv': jax.random.normal(ks[3], (2 * inner, D), dtype=jnp.float32) * D ** (-0.5), 'Wout': jax.random.normal(ks[4], (D, inner), dtype=jnp.float32) * inner ** (-0.5), 'b_out': jnp.zeros((D,), dtype=jnp.float32)}
    _L0_xattn_all = _L0_xattn_setup()
    _L0_xattn_in = {k: v for k, v in _L0_xattn_all.items() if k in ('Wq', 'Wkv', 'Wout', 'b_out')}
    del _L0_xattn_all

    def _L0_ffn_setup():
        import math
        import jax, jax.numpy as jnp
        import numpy as np
        B, S, H, I, E = (4, 512, 256, 1024, 8)
        CAPACITY_FACTOR = 1.0
        key = jax.random.key(seed)
        k1, k2, k3, k4, k5 = jax.random.split(key, 5)
        x = jax.random.normal(k1, (B, S, H), dtype=jnp.float32)
        limit = math.sqrt(6.0 / (H + E))
        router_w = jax.random.uniform(k2, (E, H), dtype=jnp.float32, minval=-limit, maxval=limit)
        router_b = jnp.zeros((E,), dtype=jnp.float32)
        experts_inter = jax.random.normal(k3, (E, H, I), dtype=jnp.float32) * 0.02
        experts_out = jax.random.normal(k4, (E, I, H), dtype=jnp.float32) * 0.02
        return {'x': x, 'router_w': router_w, 'router_b': router_b, 'experts_inter': experts_inter, 'experts_out': experts_out}
    _L0_ffn_all = _L0_ffn_setup()
    _L0_ffn_in = {k: v for k, v in _L0_ffn_all.items() if k in ('router_w', 'router_b', 'experts_inter', 'experts_out')}
    del _L0_ffn_all
    return {'x': x, 'ctx_1024': ctx_1024, 'mask_BxS2_bf1': mask_BxS2_bf1, 'L0_attn_Wq': _L0_attn_in['Wq'], 'L0_attn_bq': _L0_attn_in['bq'], 'L0_attn_Wk': _L0_attn_in['Wk'], 'L0_attn_bk': _L0_attn_in['bk'], 'L0_attn_Wv': _L0_attn_in['Wv'], 'L0_attn_bv': _L0_attn_in['bv'], 'L0_attn_Wo': _L0_attn_in['Wo'], 'L0_attn_bo': _L0_attn_in['bo'], 'L0_attn_ln_g': _L0_attn_in['ln_g'], 'L0_attn_ln_b': _L0_attn_in['ln_b'], 'L0_xattn_Wq': _L0_xattn_in['Wq'], 'L0_xattn_Wkv': _L0_xattn_in['Wkv'], 'L0_xattn_Wout': _L0_xattn_in['Wout'], 'L0_xattn_b_out': _L0_xattn_in['b_out'], 'L0_ffn_router_w': _L0_ffn_in['router_w'], 'L0_ffn_router_b': _L0_ffn_in['router_b'], 'L0_ffn_experts_inter': _L0_ffn_in['experts_inter'], 'L0_ffn_experts_out': _L0_ffn_in['experts_out']}

def reference(x, ctx_1024, mask_BxS2_bf1, L0_attn_Wq, L0_attn_bq, L0_attn_Wk, L0_attn_bk, L0_attn_Wv, L0_attn_bv, L0_attn_Wo, L0_attn_bo, L0_attn_ln_g, L0_attn_ln_b, L0_xattn_Wq, L0_xattn_Wkv, L0_xattn_Wout, L0_xattn_b_out, L0_ffn_router_w, L0_ffn_router_b, L0_ffn_experts_inter, L0_ffn_experts_out):
    import jax
    import jax.numpy as jnp

    def _L0_attn_ref(x, Wq, bq, Wk, bk, Wv, bv, Wo, bo, ln_g, ln_b):
        import jax, jax.numpy as jnp
        import numpy as np
        C = 256
        H = 16
        K = 2
        B, N = (4, 1024)

        def _heads(t):
            shp = t.shape
            d = shp[-1] // H
            t = t.reshape(shp[:-1] + (H, d))
            return jnp.swapaxes(t, -2, -3)
        dtype = x.dtype
        q = x + jnp.einsum('bnc,cd->bnd', x, Wq) + bq
        ks = x[None] + jnp.einsum('bnc,kcd->kbnd', x, Wk) + bk[:, None, None, :]
        vs = x[None] + jnp.einsum('bnc,kcd->kbnd', x, Wv) + bv[:, None, None, :]
        q = _heads(q)
        ks = _heads(ks)
        vs = _heads(vs)
        scale = 1.0 / jnp.sqrt(jnp.asarray(N, dtype=jnp.float32))
        ks = ks.astype(jnp.float32) * scale
        vs = vs.astype(jnp.float32) * scale
        states = jnp.einsum('kbhnd,kbhne->kbhde', ks, vs)
        state = jnp.prod(states, axis=0)
        out = jnp.einsum('bhnd,bhde->bhne', q.astype(jnp.float32), state)
        out = out.astype(dtype)
        out = jnp.swapaxes(out, 1, 2).reshape(x.shape[0], x.shape[1], C)
        mu = jnp.mean(out, axis=-1, keepdims=True)
        var = jnp.var(out, axis=-1, keepdims=True)
        out = (out - mu) / jnp.sqrt(var + 1e-05) * ln_g + ln_b
        out = jnp.einsum('bnc,cd->bnd', out, Wo) + bo
        return out

    def _L0_xattn_ref(x, context, mask, Wq, Wkv, Wout, b_out):
        import jax, jax.numpy as jnp
        import numpy as np
        HEADS = 16
        DIM_HEAD = 64
        SCALE = DIM_HEAD ** (-0.5)
        B, Nq, _ = x.shape
        Nkv = context.shape[1]
        q = x @ Wq.T
        kv = context @ Wkv.T
        k, v = jnp.split(kv, 2, axis=-1)
        q = q.reshape(B, Nq, HEADS, DIM_HEAD).transpose(0, 2, 1, 3)
        k = k.reshape(B, Nkv, HEADS, DIM_HEAD).transpose(0, 2, 1, 3)
        v = v.reshape(B, Nkv, HEADS, DIM_HEAD).transpose(0, 2, 1, 3)
        sim = jnp.einsum('bhid,bhjd->bhij', q, k) * SCALE
        max_neg = -jnp.finfo(sim.dtype).max
        sim = jnp.where(mask[:, None, None, :], sim, max_neg)
        attn = jax.nn.softmax(sim, axis=-1)
        out = jnp.einsum('bhij,bhjd->bhid', attn, v)
        out = out.transpose(0, 2, 1, 3).reshape(B, Nq, HEADS * DIM_HEAD)
        return out @ Wout.T + b_out

    def _L0_ffn_ref(x, router_w, router_b, experts_inter, experts_out):
        import math
        import jax, jax.numpy as jnp
        import numpy as np
        B, S, H, I, E = (4, 512, 256, 1024, 8)
        CAPACITY_FACTOR = 1.0
        b, s, h = x.shape
        e = experts_inter.shape[0]
        capacity = math.ceil(b * s / e * CAPACITY_FACTOR)
        routing_weights = jax.nn.softmax(x @ router_w.T + router_b, axis=-1)
        x_flat = x.reshape(-1, h)
        w_flat = routing_weights.reshape(-1, e)
        routing_mask = (w_flat > 0).astype(jnp.int32)
        sorted_indices = jnp.argsort(-routing_mask, axis=0, stable=True)
        sorted_mask = jnp.take_along_axis(routing_mask, sorted_indices, axis=0)[:capacity]
        sorted_indices = sorted_indices[:capacity]
        used_tokens_indices = (sorted_indices * sorted_mask).reshape(-1)
        mask_f = sorted_mask.reshape(-1).astype(x.dtype)[:, None]
        inputs_tokens = x_flat[used_tokens_indices] * mask_f
        inputs_tokens = inputs_tokens.reshape(capacity, e, h)
        inputs_weights = jnp.take_along_axis(w_flat, sorted_indices, axis=0)
        inter = jnp.einsum('ceh,ehi->cei', inputs_tokens, experts_inter)
        inter = jax.nn.relu(inter)
        out = jnp.einsum('cei,eih->ceh', inter, experts_out)
        out = out * inputs_weights[..., None]
        out = out.reshape(-1, h)
        combined = jnp.zeros_like(x_flat).at[used_tokens_indices].add(out)
        return combined.reshape(b, s, h)
    x = _layernorm(x + _L0_attn_ref(x, L0_attn_Wq, L0_attn_bq, L0_attn_Wk, L0_attn_bk, L0_attn_Wv, L0_attn_bv, L0_attn_Wo, L0_attn_bo, L0_attn_ln_g, L0_attn_ln_b), axis=-1)
    x = _layernorm(x + _L0_xattn_ref(x, ctx_1024, mask_BxS2_bf1, L0_xattn_Wq, L0_xattn_Wkv, L0_xattn_Wout, L0_xattn_b_out), axis=-1)
    x = _layernorm(x + _L0_ffn_ref(x, L0_ffn_router_w, L0_ffn_router_b, L0_ffn_experts_inter, L0_ffn_experts_out), axis=-1)
    return x

_drawn_inputs = setup_inputs


def setup_inputs(seed=0):
    import zlib

    import numpy as np

    out = dict(_drawn_inputs(seed))
    spreads = {'L0_attn_bq': (0.0, 0.1),
     'L0_attn_bk': (0.0, 0.732),
     'L0_attn_bv': (0.0, 0.729),
     'L0_attn_bo': (0.0, 0.1),
     'L0_attn_ln_g': (1.0, 0.2),
     'L0_attn_ln_b': (0.0, 0.1),
     'L0_xattn_b_out': (0.0, 0.1),
     'L0_ffn_router_b': (0.0, 0.8)}
    factors = {}
    for name, (base, spread) in spreads.items():
        noise = np.random.default_rng([zlib.crc32(name.encode()), seed]).standard_normal(out[name].shape)
        drawn = base * np.exp(spread * noise) if base else spread * noise
        out[name] = jnp.asarray(drawn.astype(out[name].dtype))
    for name, factor in factors.items():
        out[name] = (out[name] * factor).astype(out[name].dtype)
    return out
```

```python
from contextlib import ExitStack

import concourse.bass as bass
from concourse import mybir
from concourse.alu_op_type import AluOpType as ALU

ACT = mybir.ActivationFunctionType
AX = mybir.AxisListType
F32 = mybir.dt.float32
F32R = mybir.dt.float32r
BF16 = mybir.dt.bfloat16
I32 = mybir.dt.int32

P = 128
EPS = 1e-5


def f32(ap):
    return ap.bitcast(F32)


def build(nc, t):
    NB, S, C = t["x"].shape
    NKV = t["ctx_1024"].shape[1]
    INNER = t["L0_xattn_Wq"].shape[0]
    E, _, FF = t["L0_ffn_experts_inter"].shape
    MC = C // P
    TPB = S // P
    PAIRS = INNER // P
    KEYS = 2 * PAIRS * NKV
    HEADS = 2 * PAIRS
    assert (MC, TPB, PAIRS, NKV) == (2, 4, 8, 64)
    TOK = NB * S
    CAP = TOK // E
    GT_ = CAP // P
    GROUPS = TOK // CAP
    FC = FF // P

    kv_scr = nc.dram_tensor("kv_scratch", (2, NB, P, PAIRS, NKV), F32).ap()
    x2_scr = nc.dram_tensor("x2_scratch", (TOK, C), F32).ap()
    out_rows = t["out"].rearrange("b s c -> (b s) c")

    with ExitStack() as whole:
        keep = Names(nc, whole)
        setup_and_attention(nc, t, keep, kv_scr, x2_scr, out_rows,
                            NB, S, C, NKV, MC, TPB, PAIRS, KEYS, HEADS)
    with ExitStack() as whole:
        ffn(nc, t, Names(nc, whole), x2_scr, out_rows, C, MC, E, FF, FC, CAP, GT_, GROUPS)


class Names:

    def __init__(self, nc, stack):
        self.nc, self.stack = nc, stack

    def sb(self, name, shape, dt=F32):
        return self.stack.enter_context(self.nc.sbuf_tensor(name, shape, dt))

    def ps(self, name, shape=(P, 512), dt=F32):
        return self.stack.enter_context(self.nc.psum_tensor(name, list(shape), dt))

    def sem(self, name):
        return self.stack.enter_context(self.nc.semaphore(name))


class Counted:

    def __init__(self, eng, sem, name, step=1):
        self.eng, self.sem, self.step = eng, sem, step
        self.value = eng.alloc_register(name)
        self.last = 0

    def enter_loop(self):
        self.eng.reg_mov(self.value, self.last + self.step)

    def wait_next(self, value):
        if isinstance(value, int):
            self.eng.wait_ge(self.sem, value)
            self.last = value
        else:
            self.eng.wait_ge(self.sem, self.value)
            self.eng.reg_add(self.value, self.value, self.step)


def three_passes(pe, out, lhs, rhs, first, last):
    (lh, ll), (rh, rl) = lhs, rhs
    pe.matmul(out, lh, rh, start=first, stop=False)
    pe.matmul(out, lh, rl, start=False, stop=False)
    return pe.matmul(out, ll, rh, start=False, stop=last)


def setup_and_attention(nc, t, k, kv_scr, x2_scr, out_rows,
                        NB, S, C, NKV, MC, TPB, PAIRS, KEYS, HEADS):
    HK = KEYS // 2
    wv = k.sb("wv", [P, MC, 2, C])
    wk = k.sb("wk", [P, MC, 2, C])
    wqT = k.sb("wqT", [P, MC, C])
    woc = k.sb("woc", [P, MC, C])
    bvbc = k.sb("bvbc", [P, 2, C])
    bkbc = k.sb("bkbc", [P, 2, C])
    bprime = k.sb("bprime", [P, C])
    boutbc = k.sb("boutbc", [P, C])
    ident = k.sb("ident", [P, P])
    blockmask = k.sb("blockmask", [P, P])
    wqx_hi = k.sb("wqx_hi", [P, PAIRS, C], F32R)
    wqx_lo = k.sb("wqx_lo", [P, PAIRS, C], F32R)
    wox_hi = k.sb("wox_hi", [P, PAIRS, C], F32R)
    wox_lo = k.sb("wox_lo", [P, PAIRS, C], F32R)
    bq = k.sb("bq", [P, MC])
    bvsum = k.sb("bvsum", [P, 2, MC])
    maskrow = k.sb("maskrow", [1, NB * NKV], BF16)
    ones_bf = k.sb("ones_bf", [1, P], BF16)
    ones33 = k.sb("ones33", [33, P], F32R)
    epsc = k.sb("epsc", [P, 2])

    xraw = k.sb("xraw", [P, 2, TPB, C + 1])
    kraw = k.sb("kraw", [P, PAIRS, P])
    vraw = k.sb("vraw", [P, PAIRS, P])
    rows = k.sb("rows", [33, 2 * C], F32R)

    with ExitStack() as st:
        setup(nc, t, Names(nc, st), kv_scr, NB, S, C, NKV, MC, PAIRS,
              wv, wk, wqT, woc, bvbc, bkbc, bprime, boutbc, ident, blockmask,
              wqx_hi, wqx_lo, wox_hi, wox_lo, bq, bvsum, maskrow, ones_bf, ones33, epsc,
              xraw, kraw, vraw, rows)

    xT_hi = k.sb("xT_hi", [P, 2, MC, P], F32R)
    xT_lo = k.sb("xT_lo", [P, 2, MC, P], F32R)
    xb = k.sb("xb", [P, 2, C])
    x1 = k.sb("x1", [P, 2, TPB, C])
    x1T_hi = k.sb("x1T_hi", [P, TPB, MC, P], F32R)
    x1T_lo = k.sb("x1T_lo", [P, TPB, MC, P], F32R)
    g_sb = k.sb("g_sb", [P, 2 * C + 2 - P])
    g10 = k.sb("g10", [P, P])
    t_sb = k.sb("t_sb", [P, MC, 2, C])
    r_sb = k.sb("r_sb", [P, 2, MC])
    s01 = k.sb("s01", [P, 2, MC, P])
    sprod = k.sb("sprod", [P, MC, P])
    sbdT = k.sb("sbdT", [P, MC, P])
    sbd = k.sb("sbd", [P, MC, P])
    sw = k.sb("sw", [P, MC, C])
    mmw_hi = k.sb("mmw_hi", [P, MC, 2 * C], F32R)
    mmw_lo = k.sb("mmw_lo", [P, MC, 2 * C], F32R)
    a_hi = k.sb("a_hi", [P, MC, KEYS], F32R)
    a_lo = k.sb("a_lo", [P, MC, KEYS], F32R)
    b_hi = k.sb("b_hi", [P, PAIRS, C], F32R)
    b_lo = k.sb("b_lo", [P, PAIRS, C], F32R)
    k_hi = k.sb("k_hi", [P, PAIRS, P], F32R)
    k_lo = k.sb("k_lo", [P, PAIRS, P], F32R)
    v_hi = k.sb("v_hi", [P, PAIRS, P], F32R)
    v_lo = k.sb("v_lo", [P, PAIRS, P], F32R)
    prob = k.sb("prob", [P, 2, KEYS])
    mx = k.sb("mx", [P, HEADS])
    zsum = k.sb("zsum", [P, HEADS])
    rz = k.sb("rz", [P, 2, HEADS])
    pT_hi = k.sb("pT_hi", [P, PAIRS, P], F32R)
    pT_lo = k.sb("pT_lo", [P, PAIRS, P], F32R)
    h1 = k.sb("h1", [P, 2, C])
    h2 = k.sb("h2", [P, 2, C])
    x2 = k.sb("x2", [P, 4, C])
    o_sb = k.sb("o_sb", [P, 4, C])
    bst = k.sb("bst", [P, 4, 2, 6])
    mv = k.sb("mv", [P, 4, 2, 2])
    ve = k.sb("ve", [P, 4, 2])
    rstd = k.sb("rstd", [P, 4, 2])
    nmr = k.sb("nmr", [P, 4, 2])

    sim = [k.ps("sim0"), k.ps("sim1")]
    pt = [k.ps("pt0"), k.ps("pt1")]
    zb = k.ps("zb")
    ob = k.ps("ob")
    tr = k.ps("tr")
    pw = k.ps("pw")

    s = {n: k.sem(n) for n in (
        "x_loaded", "k_loaded", "v_loaded",
        "prep_made", "prep_hi", "prep_taken", "state_made", "state_ready", "st_prod",
        "k_hi_made", "k_lo_made", "v_hi_made", "v_lo_made",
        "tr_made", "tr_hi", "tr_taken", "xb_ready",
        "z_made", "z_taken", "h1_made", "x1_ready", "x1_biased",
        "sim_made", "max_made", "sim_taken", "exp_made", "sum_made", "rz_made", "p_ready",
        "pt_made", "pt_hi_made", "pt_taken", "o_made", "o_taken",
        "x2_ready", "out_ready", *(f"x2_stored{i}" for i in range(4)), *(f"out_stored{i}" for i in range(4)),
        "bst0", "bst1", "bst2", "bst3", "mv0", "mv1", "mv2", "mv3",
        "ve0", "ve1", "ve2", "ve3", "rstd0", "rstd1", "rstd2", "rstd3", "nmr1", "nmr2", "nmr3")}
    NTILES = NB * TPB

    ORDER = [("MW", 0, "a"), ("G", 0, "b"), ("GT", 0, "c"), ("B0", 0, "f"),
             ("B1", 1, "a"), ("B2", 1, "b"), ("B3", 1, "c"), ("T0", 1, "d"), ("T1", 1, "e"), ("R", 1, "f"),
             ("ST", 2, "a"), ("SW", 2, "d"), ("SB", 2, "e"),
             ("A0", 3, "a"), ("A1", 3, "b"), ("A2", 3, "c"), ("A3", 3, "d"), ("ROW", 3, "e"), ("M", 3, "f")]

    def batch_of(name, it):
        return it + (1 if name[0] == "A" or name == "MW" else 0 if name[0] == "B" else 2)

    def enabled(name, it):
        return not isinstance(it, int) or 0 <= batch_of(name, it) < NB

    def count(it):
        return sum(enabled(n, it) for n, _, _ in ORDER)

    BEFORE0 = count(-2) + count(-1)

    def prep_no(it, name):
        names = [n for n, _, _ in ORDER]
        if isinstance(it, int):
            before = sum(count(i) for i in range(-2, it))
            return before + sum(enabled(n, it) for n in names[:names.index(name) + 1])
        return it * len(ORDER) + BEFORE0 + names.index(name) + 1

    def at(slot, place, it):
        return [n for n, sl, pl in ORDER if (sl, pl) == (slot, place) and enabled(n, it)]

    def within(b):
        return not isinstance(b, int) or 0 <= b < NB

    def need(eng, name, value):
        if not isinstance(value, int) or value > 0:
            eng.wait_ge(s[name], value)

    def xT_no(n):
        return 1 if isinstance(n, int) and n == 0 else 2 * n

    def x1T_no(n):
        return 2 * n + 3 - (1 if isinstance(n, int) and n == NTILES - 1 else 0)

    counted = {}
    half = lambda buf, h: buf[:, :, h * HK:(h + 1) * HK]

    block = k.stack.enter_context(nc.Block())

    def sp_slot(sp, it, slot, e):
        if slot == 0 and within(it + 1):
            need(sp, "k_lo_made", it + 1)
            load_kv(sp, kraw, 0, it + 1, "k_loaded")
        if slot == 1 and within(it + 1):
            need(sp, "v_lo_made", it + 1)
            load_kv(sp, vraw, 1, it + 1, "v_loaded")
        if slot == 3 and within(it + 3):
            need(sp, "x_loaded", 16 * (it + 3))
            need(sp, "tr_made", xT_no(4 * (it + 2) - 1))
            need(sp, "xb_ready", 4 * (it + 2))
            sp.dma_start(xraw[:, (e + 1) % 2, :, 0:C], x_tiles(it + 3)).then_inc(s["x_loaded"], 16)
        n = 4 * it + slot
        if tile_exists(n - 2):
            store(sp, n - 2, (slot - 2) % 4, o_sb, "out_ready", "out_stored", out_rows)
        if tile_exists(n - 1):
            store(sp, n - 1, (slot - 1) % 4, x2, "x2_ready", "x2_stored", x2_scr)

    def tile_exists(n):
        return not isinstance(n, int) or 0 <= n < NTILES

    def store(sp, n, b, buf, ready, stored, dram):
        need(sp, ready, n + 1)
        rows_of = dram[n * P:(n + 1) * P, :] if isinstance(n, int) else dram[bass.ds(n * P, P), :]
        sp.dma_start(rows_of, buf[:, b, :]).then_inc(s[f"{stored}{b}"], 16)

    def x_tiles(b):
        if isinstance(b, int):
            return t["x"][b].rearrange("(i p) c -> p i c", p=P)
        return t["x"][bass.ds(b, 1), :, :].rearrange("o (i p) c -> p (o i) c", p=P)

    def load_kv(sp, dst, which, b, sem):
        for h in range(2):
            q = slice(64 * h, 64 * h + 64)
            if isinstance(b, int):
                src = kv_scr[which, b, q, :, :]
            else:
                src = kv_scr[which, bass.ds(b, 1), q, :, :].rearrange("o p r j -> (o p) r j")
            sp.dma_start(dst[q, :, 64 * h:64 * h + 64], src).then_inc(s[sem], 16)

    def pe_prep(pe, name, it, q):
        b = batch_of(name, it)
        n = prep_no(it, name)
        need(pe, "prep_taken", n - 1)
        i = int(name[-1]) if name[-1].isdigit() else 0
        if name == "G":
            need(pe, "x_loaded", 16 * (b + 1))
            for m, (lo_c, o) in enumerate(((0, 0), (P, C + 1))):
                for tile in range(TPB):
                    last = pe.matmul(pw[:, o:o + C + 1 - lo_c], xraw[:, q, tile, m * P:(m + 1) * P],
                                     xraw[:, q, tile, lo_c:C + 1], start=tile == 0, stop=tile == TPB - 1)
        elif name == "GT":
            last = pe.transpose(pw[:, 0:P], g_sb[:, P:C], ident[:, :])
        elif name[0] == "T":
            lhs = (g_sb[:, 0:P], g10[:, :]) if i == 0 else (g_sb[:, P:C], g_sb[:, C + 1:C + 1 + P])
            for m in range(MC):
                last = pe.matmul(pw[:, :], lhs[m], wv[:, m, :, :].rearrange("p s e -> p (s e)"),
                                 start=m == 0, stop=m == MC - 1)
        elif name == "R":
            for st in range(2):
                for blk in range(MC):
                    col = st * MC + blk
                    for m in range(MC):
                        last = pe.matmul(pw[:, col:col + 1], wv[:, m, st, blk * P:(blk + 1) * P],
                                         g_sb[:, C:C + 1] if m == 0 else g_sb[:, C + 1 + P:C + 2 + P],
                                         start=m == 0, stop=m == MC - 1)
        elif name == "ST":
            for st in range(2):
                for blk in range(MC):
                    o = (st * MC + blk) * P
                    for m in range(MC):
                        last = pe.matmul(pw[:, o:o + P], t_sb[:, m, st, blk * P:(blk + 1) * P],
                                         wk[:, m, st, blk * P:(blk + 1) * P], start=m == 0, stop=m == MC - 1)
        elif name == "SW":
            need(pe, "state_ready", b + 1)
            for blk in range(MC):
                last = pe.matmul(pw[:, blk * C:(blk + 1) * C], sbdT[:, blk, :], woc[:, blk, :],
                                 start=True, stop=True)
        elif name == "SB":
            for blk in range(MC):
                last = pe.transpose(pw[:, blk * P:(blk + 1) * P], sbdT[:, blk, :], ident[:, :])
        elif name == "ROW":
            for blk in range(MC):
                pe.matmul(pw[0:1, blk * P:(blk + 1) * P], bq[:, blk:blk + 1], sbd[:, blk, :],
                          start=True, stop=True)
            for blk in range(MC):
                last = pe.matmul(pw[0:1, C:2 * C], bq[:, blk:blk + 1], sw[:, blk, :],
                                 start=blk == 0, stop=blk == MC - 1)
        elif name == "M":
            for m in range(MC):
                for blk in range(MC):
                    o = m * C + blk * P
                    last = pe.matmul(pw[:, o:o + P], wqT[:, blk, m * P:(m + 1) * P], sbd[:, blk, :],
                                     start=True, stop=True)
        elif name == "MW":
            for m in range(MC):
                for blk in range(MC):
                    last = pe.matmul(pw[:, m * C:(m + 1) * C], wqT[:, blk, m * P:(m + 1) * P], sw[:, blk, :],
                                     start=blk == 0, stop=blk == MC - 1)
        elif name[0] == "A":
            if i == 0:
                need(pe, "k_hi_made", b + 1)
                need(pe, "k_lo_made", b + 1)
            m, hf = i % 2, i // 2
            for r in range(PAIRS // 2):
                pr = hf * (PAIRS // 2) + r
                c = slice(m * P, (m + 1) * P)
                last = three_passes(pe, pw[:, r * P:(r + 1) * P], (wqx_hi[:, pr, c], wqx_lo[:, pr, c]),
                                    (k_hi[:, pr, :], k_lo[:, pr, :]), True, True)
        else:
            if i == 0:
                need(pe, "v_hi_made", b + 1)
                need(pe, "v_lo_made", b + 1)
            for r in range(2):
                pr = 2 * i + r
                last = three_passes(pe, pw[:, r * C:(r + 1) * C], (v_hi[:, pr, :], v_lo[:, pr, :]),
                                    (wox_hi[:, pr, :], wox_lo[:, pr, :]), True, True)
        last.then_inc(s["prep_made"], 1)

    def pe_x1T(pe, n, slot, q):
        need(pe, "tr_taken", x1T_no(n) - 1)
        need(pe, "x1_ready", n + 1)
        for m in range(MC):
            last = pe.transpose(tr[:, m * P:(m + 1) * P], x1[:, q, slot, m * P:(m + 1) * P], ident[:, :])
        last.then_inc(s["tr_made"], 1)

    def pe_xT(pe, n, b, slot, q):
        need(pe, "tr_taken", xT_no(n) - 1)
        need(pe, "x_loaded", 16 * (b + 1))
        for m in range(MC):
            last = pe.transpose(tr[:, m * P:(m + 1) * P], xraw[:, q, slot, m * P:(m + 1) * P], ident[:, :])
        last.then_inc(s["tr_made"], 1)

    def pe_sim(pe, it, slot, h):
        n = 4 * it + slot
        if h == 0:
            need(pe, "sim_taken", n)
            need(pe, "tr_taken", x1T_no(n))
            if slot == 0:
                need(pe, "prep_taken", prep_no(it - 1, "A3"))
        for m in range(MC):
            three_passes(pe, sim[h][:, :], (x1T_hi[:, slot, m, :], x1T_lo[:, slot, m, :]),
                         (half(a_hi, h)[:, m, :], half(a_lo, h)[:, m, :]), m == 0, False)
        row = maskrow[0:1, it * NKV:(it + 1) * NKV] if isinstance(it, int) else maskrow[0:1, bass.ds(it * NKV, NKV)]
        last = pe.matmul(sim[h][:, :].rearrange("p (g j) -> p g j", j=NKV), ones_bf[:, :],
                         row.unsqueeze(1).broadcast_to([1, HEADS // 2, NKV]), start=False, stop=True)
        last.then_inc(s["sim_made"], 1)

    def pe_pT(pe, n, par_n):
        need(pe, "p_ready", n + 1)
        for h in range(2):
            need(pe, "pt_taken", 2 * (n - 1) + h + 1)
            for r in range(PAIRS // 2):
                c = (h * (PAIRS // 2) + r) * P
                last = pe.transpose(pt[h][:, r * P:(r + 1) * P], prob[:, par_n, c:c + P], ident[:, :])
            last.then_inc(s["pt_made"], 1)

    def pe_pB(pe, n, it, slot, h):
        need(pe, "pt_taken", 2 * n + h + 1)
        if h == 0:
            need(pe, "o_taken", n)
        if slot == 0:
            need(pe, "prep_taken", prep_no(it, "B1" if h == 0 else "B3"))
        for r in range(PAIRS // 2):
            pr = h * (PAIRS // 2) + r
            last = three_passes(pe, ob[:, 0:C], (pT_hi[:, pr, :], pT_lo[:, pr, :]),
                                (b_hi[:, pr, :], b_lo[:, pr, :]), pr == 0, pr == PAIRS - 1)
        if h == 1:
            last.then_inc(s["o_made"], 1)

    def pe_z(pe, it, slot):
        n = 4 * (it + 1) + slot
        need(pe, "z_taken", n)
        need(pe, "tr_taken", xT_no(n))
        if slot == 0:
            need(pe, "prep_taken", prep_no(it, "MW"))
        for m in range(MC):
            three_passes(pe, zb[:, :], (xT_hi[:, slot % 2, m, :], xT_lo[:, slot % 2, m, :]),
                         (mmw_hi[:, m, :], mmw_lo[:, m, :]), m == 0, False)
        pe.matmul(zb[:, :], ones33[:, :], rows[:, :], start=False, stop=True).then_inc(s["z_made"], 1)

    def parts(it, slot):
        n = 4 * it + slot
        isint = isinstance(it, int)
        has_sim = not isint or 0 <= it < NB
        has_z = not isint or 0 <= it + 1 < NB
        has_prev = not isint or 1 <= n <= NTILES
        has_xT = not isint or 0 <= n + 5 < NTILES
        has_x1T = not isint or 0 <= n + 3 < NTILES
        return has_sim, has_z, has_prev, has_xT, has_x1T

    def pe_slot(pe, it, slot, e):
        par = lambda a: (e + a) % 2
        has_sim, has_z, has_prev, has_xT, has_x1T = parts(it, slot)
        n = 4 * it + slot
        prep = lambda place: [pe_prep(pe, x, it, par(0)) for x in at(slot, place, it)]
        if has_sim:
            pe_sim(pe, it, slot, 0)
        if has_x1T:
            pe_x1T(pe, n + 3, (slot - 1) % 4, par(1 if slot else 0))
        prep("a")
        if has_sim:
            pe_sim(pe, it, slot, 1)
        prep("b")
        if has_prev:
            pe_pT(pe, n - 1, (slot - 1) % 2)
        if has_z:
            pe_z(pe, it, slot)
        prep("c")
        if has_xT:
            pe_xT(pe, n + 5, it + 1 if slot < 3 else it + 2, (slot + 1) % 4, par(1 if slot < 3 else 2))
        prep("d")
        if has_prev:
            pe_pB(pe, n - 1, it if slot else it - 1, (slot - 1) % 4, 0)
        prep("e")
        if has_prev:
            pe_pB(pe, n - 1, it if slot else it - 1, (slot - 1) % 4, 1)
        prep("f")

    def prep_views(name):
        i = int(name[-1]) if name[-1].isdigit() else 0
        by_m = lambda buf: buf.rearrange("p (m e) -> p m e", m=MC)
        if name == "G":
            return pw[:, 0:2 * C + 2 - P], g_sb[:, :], None
        if name == "GT":
            return pw[:, 0:P], g10[:, :], None
        if name == "SW":
            return by_m(pw[:, :]), sw[:, :, :], None
        if name == "SB":
            return by_m(pw[:, 0:MC * P]), sbd[:, :, :], None
        if name == "ROW":
            return pw[0:1, :], rows[0:1, :], rows[32:33, :]
        if name == "M":
            return by_m(pw[:, :]), mmw_hi[:, :, 0:C], mmw_lo[:, :, 0:C]
        if name == "MW":
            return by_m(pw[:, :]), mmw_hi[:, :, C:2 * C], mmw_lo[:, :, C:2 * C]
        if name[0] == "A":
            return pw[:, :], half(a_hi, i // 2)[:, i % 2, :], half(a_lo, i // 2)[:, i % 2, :]
        return (pw[:, :].rearrange("p (r c) -> p r c", r=2), b_hi[:, 2 * i:2 * i + 2, :],
                b_lo[:, 2 * i:2 * i + 2, :])

    SPLIT = ("A0", "A1", "A2", "A3", "B0", "B1", "B2", "B3", "M", "MW", "ROW")
    COPY = ("G", "GT", "SW", "SB")

    def split_no(it, name):
        names = [n for n, _, _ in ORDER if n in SPLIT]
        if isinstance(it, int):
            return (sum(enabled(n, i) for i in range(-2, it) for n in names)
                    + sum(enabled(n, it) for n in names[:names.index(name) + 1]))
        before = sum(enabled(n, i) for i in range(-2, 0) for n in names)
        return it * len(names) + before + names.index(name) + 1

    def act_prep(act, name, it):
        if name in COPY + SPLIT:
            src, dst, _ = prep_views(name)
            need(act, "prep_made", prep_no(it, name))
            act.activation(dst, src, ACT.Copy).then_inc(
                s["prep_hi" if name in SPLIT else "prep_taken"], 1)

    def act_norm(act, ln, q, src, dst, done):
        act.activation(dst, src, ACT.Identity, bias=nmr[:, ln, q:q + 1], scale=rstd[:, ln, q:q + 1]).then_inc(s[done], 1)

    def act_slot(act, it, slot, e):
        par = lambda a: (e + a) % 2
        has_sim, has_z, has_prev, has_xT, has_x1T = parts(it, slot)
        n = 4 * it + slot
        q = slot % 2
        prep = lambda place: [act_prep(act, x, it) for x in at(slot, place, it)]
        if slot == 1 and within(it + 1):
            need(act, "k_loaded", 32 * (it + 2))
            if within(it):
                need(act, "prep_made", prep_no(it - 1, "A3"))
            act.activation(k_hi[:, :, :], kraw[:, :, :], ACT.Copy).then_inc(s["k_hi_made"], 1)
        if slot == 2 and within(it + 1):
            need(act, "v_loaded", 32 * (it + 2))
            if within(it):
                need(act, "prep_made", prep_no(it, "B3"))
            act.activation(v_hi[:, :, :], vraw[:, :, :], ACT.Copy).then_inc(s["v_hi_made"], 1)
        if has_x1T:
            need(act, "tr_made", x1T_no(n + 3))
            act.activation(x1T_hi[:, (slot - 1) % 4, :, :], tr[:, 0:C].rearrange("p (m u) -> p m u", m=MC),
                           ACT.Copy).then_inc(s["tr_hi"], 1)
        prep("a")
        prep("b")
        if has_prev:
            for h in range(2):
                need(act, "pt_made", 2 * (n - 1) + h + 1)
                act.activation(pT_hi[:, h * 4:h * 4 + 4, :], pt[h][:, :].rearrange("p (r u) -> p r u", u=P),
                               ACT.Copy).then_inc(s["pt_hi_made"], 1)
        if has_sim:
            need(act, "sim_taken", n + 1)
            act.activation(prob[:, q, :], prob[:, q, :], ACT.Exp).then_inc(s["exp_made"], 1)
        prep("c")
        if has_xT:
            need(act, "tr_made", xT_no(n + 5))
            act.activation(xT_hi[:, (slot + 1) % 2, :, :], tr[:, 0:C].rearrange("p (m u) -> p m u", m=MC),
                           ACT.Copy).then_inc(s["tr_hi"], 1)
        prep("d")
        prep("e")
        if has_z:
            need(act, "nmr1", n + 5)
            need(act, "o_taken", n - 3)
            act_norm(act, 1, q, h1[:, q, :], x1[:, par(1), slot, :], "x1_ready")
        prep("f")
        if tile_exists(n - 2):
            need(act, "nmr3", n - 1)
            need(act, f"out_stored{(slot - 2) % 4}", 16 * (it if slot >= 2 else it - 1))
            act_norm(act, 3, q, x2[:, (slot - 2) % 4, :], o_sb[:, (slot - 2) % 4, :], "out_ready")
        if has_prev:
            need(act, "nmr2", n)
            need(act, f"x2_stored{(slot - 1) % 4}", 16 * (it if slot >= 1 else it - 1))
            act_norm(act, 2, 1 - q, h2[:, 1 - q, :], x2[:, (slot - 1) % 4, :], "x2_ready")

    def dve_prep(dve, name, it):
        n = prep_no(it, name)
        if name in SPLIT:
            src, hi, lo = prep_views(name)
            need(dve, "prep_hi", split_no(it, name))
            dve.tensor_tensor(lo, src, f32(hi), ALU.subtract).then_inc(s["prep_taken"], 1)
        elif name[0] == "T":
            m = int(name[1])
            need(dve, "prep_made", n)
            col = g_sb[:, C:C + 1] if m == 0 else g_sb[:, C + 1 + P:C + 2 + P]
            dve.scalar_tensor_tensor(t_sb[:, m, :, :].rearrange("p s e -> p (s e)"),
                                     bvbc[:, :, :].rearrange("p s e -> p (s e)"), col, pw[:, :],
                                     ALU.mult, ALU.add).then_inc(s["prep_taken"], 1)
        elif name == "R":
            need(dve, "prep_made", n)
            dve.tensor_tensor(r_sb[:, :, :].rearrange("p s b -> p (s b)"), pw[:, 0:2 * MC],
                              bvsum[:, :, :].rearrange("p s b -> p (s b)"), ALU.add).then_inc(s["prep_taken"], 1)
        elif name == "ST":
            need(dve, "prep_made", n)
            for st in range(2):
                for blk in range(MC):
                    o = (st * MC + blk) * P
                    last = dve.scalar_tensor_tensor(
                        s01[:, st, blk, :], bkbc[:, st, blk * P:(blk + 1) * P], r_sb[:, st, blk:blk + 1],
                        pw[:, o:o + P], ALU.mult, ALU.add)
            last.then_inc(s["prep_taken"], 1)

    def dve_stats(dve, ln, n, q, src):
        need(dve, f"rstd{ln}", n - 1)
        if ln:
            need(dve, f"nmr{ln}", n - 1)
        dve.bn_stats(bst[:, ln, q, :], src).then_inc(s[f"bst{ln}"], 1)
        counted[f"bst{ln}"].wait_next(n + 1)
        dve.bn_aggr(mv[:, ln, q, :], bst[:, ln, q, :]).then_inc(s[f"mv{ln}"], 1)

    def dve_slot(dve, it, slot, e):
        par = lambda a: (e + a) % 2
        has_sim, has_z, has_prev, has_xT, has_x1T = parts(it, slot)
        n = 4 * it + slot
        q = slot % 2
        prep = lambda place: [dve_prep(dve, x, it) for x in at(slot, place, it)]
        if has_x1T:
            need(dve, "tr_hi", x1T_no(n + 3))
            d = (slot - 1) % 4
            dve.tensor_tensor(x1T_lo[:, d, :, :], tr[:, 0:C].rearrange("p (m u) -> p m u", m=MC),
                              f32(x1T_hi[:, d, :, :]), ALU.subtract).then_inc(s["tr_taken"], 1)
        prep("a")
        if has_sim:
            for h in range(2):
                need(dve, "sim_made", 2 * n + h + 1)
                dve.tensor_reduce(mx[:, h * 8:h * 8 + 8], sim[h][:, :].rearrange("p (g j) -> p g j", j=NKV),
                                  AX.X, ALU.max).then_inc(s["max_made"], 1)
            dve.wait_ge(s["max_made"], 2 * n + 2)
            for h in range(2):
                last = dve.tensor_tensor(prob[:, q, h * HK:(h + 1) * HK].rearrange("p (g j) -> p g j", j=NKV),
                                         sim[h][:, :].rearrange("p (g j) -> p g j", j=NKV),
                                         mx[:, h * 8:h * 8 + 8].unsqueeze(2).broadcast_to([P, 8, NKV]),
                                         ALU.subtract)
            last.then_inc(s["sim_taken"], 1)
        prep("b")
        if has_prev:
            for h in range(2):
                need(dve, "pt_hi_made", 2 * (n - 1) + h + 1)
                dve.tensor_tensor(pT_lo[:, h * 4:h * 4 + 4, :], pt[h][:, :].rearrange("p (r u) -> p r u", u=P),
                                  f32(pT_hi[:, h * 4:h * 4 + 4, :]), ALU.subtract).then_inc(s["pt_taken"], 1)
        if has_z:
            need(dve, "z_made", n + 5)
            dve_stats(dve, 0, n + 4, q, zb[:, 0:C])
        prep("c")
        if has_xT:
            need(dve, "tr_hi", xT_no(n + 5))
            d = (slot + 1) % 2
            dve.tensor_tensor(xT_lo[:, d, :, :], tr[:, 0:C].rearrange("p (m u) -> p m u", m=MC),
                              f32(xT_hi[:, d, :, :]), ALU.subtract).then_inc(s["tr_taken"], 1)
        prep("d")
        if has_z:
            need(dve, "rstd0", n + 5)
            need(dve, "xb_ready", n + 5)
            need(dve, "x1_ready", n + 3)
            dve.scalar_tensor_tensor(h1[:, q, :], zb[:, C:2 * C], rstd[:, 0, q:q + 1], xb[:, q, :],
                                     ALU.mult, ALU.add).then_inc(s["z_taken"], 1)
            dve.wait_ge(s["z_taken"], n + 5)
            dve_stats(dve, 1, n + 4, q, h1[:, q, :])
        if has_sim:
            need(dve, "exp_made", n + 1)
            dve.tensor_reduce(zsum[:, :], prob[:, q, :].rearrange("p (g j) -> p g j", j=NKV),
                              AX.X, ALU.add).then_inc(s["sum_made"], 1)
            dve.wait_ge(s["sum_made"], n + 1)
            need(dve, "p_ready", n - 1)
            dve.reciprocal(rz[:, q, :], zsum[:, :]).then_inc(s["rz_made"], 1)
        if tile_exists(n - 2):
            need(dve, "x2_ready", n - 1)
            dve_stats(dve, 3, n - 2, q, x2[:, (slot - 2) % 4, :])
        prep("e")
        prep("f")
        if has_prev:
            need(dve, "o_made", n)
            need(dve, "x1_biased", n)
            need(dve, "x2_ready", n - 2)
            dve.tensor_tensor(h2[:, 1 - q, :], ob[:, 0:C], x1[:, par(0 if slot else -1), (slot - 1) % 4, :],
                              ALU.add).then_inc(s["o_taken"], 1)
            dve.wait_ge(s["o_taken"], n)
            dve_stats(dve, 2, n - 1, 1 - q, h2[:, 1 - q, :])

    def pool_rstd(pool, ln, n, q):
        counted[f"mv{ln}"].wait_next(n + 1)
        pool.tensor_scalar(ve[:, ln, q:q + 1], mv[:, ln, q, 1:2], EPS, None, ALU.add).then_inc(s[f"ve{ln}"], 1)
        pool.wait_ge(s[f"ve{ln}"], n + 1)
        need(pool, ("z_taken", "x1_ready", "x2_ready", "out_ready")[ln], n - 1)
        pool.tensor_tensor(rstd[:, ln, q:q + 1], ve[:, ln, q:q + 1], epsc[:, 0:1], ALU.pow).then_inc(s[f"rstd{ln}"], 1)
        if ln:
            counted[f"rstd{ln}"].wait_next(n + 1)
            pool.tensor_scalar(nmr[:, ln, q:q + 1], mv[:, ln, q, 0:1], rstd[:, ln, q:q + 1], -1.0,
                               ALU.mult, ALU.mult).then_inc(s[f"nmr{ln}"], 1)

    def pool_xb(pool, n, b, slot, q):
        need(pool, "x_loaded", 16 * (b + 1))
        need(pool, "z_taken", n - 1)
        pool.tensor_tensor(xb[:, slot % 2, :], xraw[:, q, slot, 0:C], bprime[:, :], ALU.add).then_inc(s["xb_ready"], 1)

    def pool_slot(pool, it, slot, e):
        par = lambda a: (e + a) % 2
        has_sim, has_z, has_prev, has_xT, has_x1T = parts(it, slot)
        n = 4 * it + slot
        q = slot % 2
        if has_x1T:
            need(pool, "tr_made", x1T_no(n + 3))
            pool.tensor_tensor(x1[:, par(1 if slot else 0), (slot - 1) % 4, :], x1[:, par(1 if slot else 0), (slot - 1) % 4, :], boutbc[:, :],
                               ALU.add).then_inc(s["x1_biased"], 1)
        if slot == 1 and within(it + 1):
            need(pool, "k_hi_made", it + 2)
            pool.tensor_tensor(k_lo[:, :, :], kraw[:, :, :], f32(k_hi[:, :, :]), ALU.subtract).then_inc(s["k_lo_made"], 1)
        if slot == 2 and within(it + 1):
            need(pool, "v_hi_made", it + 2)
            pool.tensor_tensor(v_lo[:, :, :], vraw[:, :, :], f32(v_hi[:, :, :]), ALU.subtract).then_inc(s["v_lo_made"], 1)
        if slot == 2 and within(it + 2):
            need(pool, "prep_taken", prep_no(it, "ST"))
            pool.tensor_tensor(sprod[:, :, :], s01[:, 0, :, :], s01[:, 1, :, :], ALU.mult).then_inc(s["st_prod"], 1)
            pool.wait_ge(s["st_prod"], it + 3)
            pool.tensor_tensor(sbdT[:, :, :], sprod[:, :, :], blockmask[:, :].unsqueeze(1).broadcast_to([P, MC, P]),
                               ALU.mult).then_inc(s["state_ready"], 1)
        if has_z:
            pool_rstd(pool, 0, n + 4, q)
            if slot < 3:
                pool_xb(pool, n + 5, it + 1, slot + 1, par(1))
            pool_rstd(pool, 1, n + 4, q)
        if slot == 3 and within(it + 2):
            pool_xb(pool, n + 5, it + 2, 0, par(2))
        if has_sim:
            need(pool, "rz_made", n + 1)
            pool.tensor_tensor(prob[:, q, :].rearrange("p (g j) -> p g j", j=NKV),
                               prob[:, q, :].rearrange("p (g j) -> p g j", j=NKV),
                               rz[:, q, :].unsqueeze(2).broadcast_to([P, HEADS, NKV]),
                               ALU.mult).then_inc(s["p_ready"], 1)
        if tile_exists(n - 2):
            pool_rstd(pool, 3, n - 2, q)
        if has_prev:
            pool_rstd(pool, 2, n - 1, 1 - q)

    FIRST, TRIPS = 1, (NB - 4) // 2

    def run(eng, slot_fn):
        for it in range(-2, FIRST):
            for slot in range(TPB):
                slot_fn(eng, it, slot, it % 2)
        for c in counted.values():
            if c.eng is eng:
                c.enter_loop()
        with eng.Fori(0, TRIPS) as i:
            for u in range(2):
                for slot in range(TPB):
                    slot_fn(eng, 2 * i + (FIRST + u), slot, (FIRST + u) % 2)
        for it in range(FIRST + 2 * TRIPS, NB + 1):
            for slot in range(TPB if it < NB else 2):
                slot_fn(eng, it, slot, it % 2)

    @block.sync
    def _(sp):
        sp.dma_start(xraw[:, 0, :, 0:C], x_tiles(0)).then_inc(s["x_loaded"], 16)
        run(sp, sp_slot)
        for i in range(4):
            sp.wait_ge(s[f"x2_stored{i}"], 16 * NB)
            sp.wait_ge(s[f"out_stored{i}"], 16 * NB)

    @block.tensor
    def _(pe):
        run(pe, pe_slot)

    @block.scalar
    def _(act):
        run(act, act_slot)

    @block.vector
    def _(dve):
        for ln in range(4):
            counted[f"bst{ln}"] = Counted(dve, s[f"bst{ln}"], f"count_bst{ln}")
        run(dve, dve_slot)

    @block.gpsimd
    def _(pool):
        for ln in range(4):
            counted[f"mv{ln}"] = Counted(pool, s[f"mv{ln}"], f"count_mv{ln}")
            if ln:
                counted[f"rstd{ln}"] = Counted(pool, s[f"rstd{ln}"], f"count_rstd{ln}")
        run(pool, pool_slot)


def setup(nc, t, k, kv_scr, NB, S, C, NKV, MC, PAIRS, wv, wk, wqT, woc, bvbc, bkbc, bprime, boutbc, ident,
          blockmask, wqx_hi, wqx_lo, wox_hi, wox_lo, bq, bvsum, maskrow, ones_bf, ones33, epsc,
          xraw, kraw, vraw, rows):
    NCTX = NB * NKV
    CT = NCTX // P
    CH = 2 * PAIRS
    W = 512
    d_head = P // 2
    wq_raw = k.sb("wq_raw", [P, MC, C])
    wo_raw = k.sb("wo_raw", [P, MC, C])
    wog = k.sb("wog", [P, MC, C])
    wout_raw = k.sb("wout_raw", [P, MC, PAIRS * P])
    wqx_raw = k.sb("wqx_raw", [P, PAIRS, C])
    wkv_raw = k.sb("wkv_raw", [P, CH, C])
    ctx_raw = k.sb("ctx_raw", [P, CT, C])
    wkvT_hi = k.sb("wkvT_hi", [P, MC, CH * P], F32R)
    wkvT_lo = k.sb("wkvT_lo", [P, MC, CH * P], F32R)
    ctxT_hi = k.sb("ctxT_hi", [P, MC, NCTX], F32R)
    ctxT_lo = k.sb("ctxT_lo", [P, MC, NCTX], F32R)
    RING = 4
    stage = k.sb("stage", [P, RING, W])
    bobc = k.sb("bobc", [P, C])
    lng = k.sb("lng", [P, MC])
    lnb = k.sb("lnb", [P, MC])
    lnb_bc = k.sb("lnb_bc", [P, MC, P])
    ones = k.sb("ones", [P, P])
    mean_w = k.sb("mean_w", [P, P])
    maskraw = k.sb("maskraw", [1, NB * NKV], mybir.dt.uint8)
    bank = [k.ps(f"su{i}") for i in range(8)]
    names = ("wq", "wo", "wv", "wk", "small", "wout", "wqx", "wkv", "ctx", "mask")
    loaded = {n: k.sem(f"{n}_loaded") for n in names}
    made, hi_made, taken = k.sem("su_made"), k.sem("su_hi"), k.sem("su_taken")
    consts, scaled, eyes, split_hi = k.sem("consts"), k.sem("scaled"), k.sem("eyes"), k.sem("split_hi")
    masked, staged = k.sem("masked"), [k.sem(f"staged{i}") for i in range(RING)]
    mask_steps = k.sem("mask_steps")

    items = [("wqT",), ("mean",), ("bprime",)]
    items += [("ctxT", m, h) for h in range(NCTX // W) for m in range(MC)]
    for g in range(CH * P // W):
        items += [("wkvT", m, g) for m in range(MC)]
    items += [("kv", ch, h) for ch in range(CH) for h in range(NCTX // W)]
    items += [("wox", g) for g in range(PAIRS // 2)]
    SPLITS = ("ctxT", "wkvT", "wox")
    col = lambda i: slice(i * P, (i + 1) * P)

    def dest(it):
        if it[0] == "ctxT":
            c = slice(it[2] * W, (it[2] + 1) * W)
            return ctxT_hi[:, it[1], c], ctxT_lo[:, it[1], c]
        if it[0] == "wkvT":
            c = slice(it[2] * W, (it[2] + 1) * W)
            return wkvT_hi[:, it[1], c], wkvT_lo[:, it[1], c]
        c = slice(2 * it[1], 2 * it[1] + 2)
        return (wox_hi[:, c, :].rearrange("p r c -> p (r c)"), wox_lo[:, c, :].rearrange("p r c -> p (r c)"))

    block = k.stack.enter_context(nc.Block())

    @block.sync
    def _(sp):
        flat = lambda ap: ap.rearrange("k c -> (k c)")
        rowbc = lambda ap, n: ap.unsqueeze(0).broadcast_to([P, n])
        sp.dma_start(ctx_raw[:, :, :], t["ctx_1024"].rearrange("b j c -> (b j) c").rearrange("(i p) c -> p i c", p=P)
                     ).then_inc(loaded["ctx"], 16)
        sp.dma_start(wkv_raw[:, :, :], t["L0_xattn_Wkv"].rearrange("(i p) c -> p i c", p=P)).then_inc(loaded["wkv"], 16)
        sp.dma_start(wout_raw[:, :, :], t["L0_xattn_Wout"].rearrange("(m p) n -> p m n", p=P)).then_inc(loaded["wout"], 16)
        sp.dma_start(wqx_raw[:, :, :], t["L0_xattn_Wq"].rearrange("(i p) c -> p i c", p=P)).then_inc(loaded["wqx"], 16)
        sp.dma_start(bvbc[:, :, :].rearrange("p s e -> p (s e)"), rowbc(flat(t["L0_attn_bv"]), 2 * C)).then_inc(loaded["small"], 16)
        sp.dma_start(bkbc[:, :, :].rearrange("p s e -> p (s e)"), rowbc(flat(t["L0_attn_bk"]), 2 * C)).then_inc(loaded["small"], 16)
        sp.dma_start(boutbc[:, :], rowbc(t["L0_xattn_b_out"], C)).then_inc(loaded["small"], 16)
        sp.dma_start(maskraw[:, :], t["mask_BxS2_bf1"].rearrange("b j -> (b j)").unsqueeze(0)).then_inc(loaded["mask"], 16)
        n = 0
        for u, it in enumerate(items):
            if it[0] == "kv":
                ch, h = it[1:]
                sp.wait_ge(taken, u + 1)
                nb = W // NKV
                sp.dma_start(kv_scr[ch // PAIRS, h * nb:(h + 1) * nb, :, ch % PAIRS, :].rearrange("b p j -> p b j"),
                             stage[:, n % RING, :].rearrange("p (b j) -> p b j", j=NKV)).then_inc(staged[n % RING], 16)
                n += 1
        for i in range(RING):
            sp.wait_ge(staged[i], 16 * (n // RING))

    @block.scalar
    def _(act):
        rowbc = lambda ap, n: ap.unsqueeze(0).broadcast_to([P, n])
        act.dma_start(wq_raw[:, :, :], t["L0_attn_Wq"].rearrange("(m p) d -> p m d", p=P)).then_inc(loaded["wq"], 16)
        act.dma_start(wo_raw[:, :, :], t["L0_attn_Wo"].rearrange("(m p) d -> p m d", p=P)).then_inc(loaded["wo"], 16)
        act.dma_start(bobc[:, :], rowbc(t["L0_attn_bo"], C)).then_inc(loaded["wo"], 16)
        with nc.allow_non_contiguous_dma(reason="a few hundred elements"):
            act.dma_start(lng[:, :], t["L0_attn_ln_g"].rearrange("(m p) -> p m", p=P)).then_inc(loaded["wo"], 16)
            act.dma_start(lnb[:, :], t["L0_attn_ln_b"].rearrange("(m p) -> p m", p=P)).then_inc(loaded["wo"], 16)
            act.dma_start(bq[:, :], t["L0_attn_bq"].rearrange("(m p) -> p m", p=P)).then_inc(loaded["small"], 16)
            act.dma_start(bvsum[:, :, :], t["L0_attn_bv"].rearrange("s (m p) -> p s m", p=P)).then_inc(loaded["small"], 16)
        for st in range(2):
            act.dma_start(wv[:, :, st, :], t["L0_attn_Wv"][st].rearrange("(m p) d -> p m d", p=P)).then_inc(loaded["wv"], 16)
            act.dma_start(wk[:, :, st, :], t["L0_attn_Wk"][st].rearrange("(m p) d -> p m d", p=P)).then_inc(loaded["wk"], 16)
        for u, it in enumerate(items):
            if it[0] in SPLITS:
                act.wait_ge(made, u + 1)
                act.activation(dest(it)[0], bank[u % 8][:, :], ACT.Copy).then_inc(hi_made, 1)
        act.wait_ge(loaded["wqx"], 16)
        act.activation(wqx_hi[:, :, :], wqx_raw[:, :, :], ACT.Copy).then_inc(split_hi, 1)

    @block.gpsimd
    def _(pool):
        pool.memset(ident[:, :], 0.0).then_inc(consts, 1)
        pool.memset(blockmask[:, :], float((2.0 ** -10) ** 2)).then_inc(consts, 1)
        pool.wait_ge(consts, 2)
        pool.affine_select(out=ident[:, :], in_=ident[:, :], compare_op=ALU.not_equal, fill=1.0, base=0,
                           pattern=[[-1, P]], channel_multiplier=1).then_inc(eyes, 1)
        groups = blockmask[:, :].rearrange("p (h e) -> p h e", e=16)
        pool.affine_select(out=groups, in_=groups, compare_op=ALU.is_ge, fill=0.0, base=0,
                           pattern=[[-16, 8], [0, 16]], channel_multiplier=1).then_inc(mask_steps, 1)
        pool.wait_ge(mask_steps, 1)
        pool.affine_select(out=groups, in_=groups, compare_op=ALU.is_ge, fill=0.0, base=15,
                           pattern=[[16, 8], [0, 16]], channel_multiplier=-1).then_inc(mask_steps, 1)
        pool.memset(epsc[:, :], -0.5)
        pool.memset(kraw[:, :, :], 0.0)
        pool.memset(vraw[:, :, :], 0.0)
        for i in range(2):
            pool.memset(xraw[:, i, :, C:C + 1], 1.0)

    @block.tensor
    def _(pe):
        pe.wait_ge(eyes, 1)
        for u, it in enumerate(items):
            b = bank[u % 8]
            if u >= 8:
                pe.wait_ge(taken, u - 7)
            kind = it[0]
            if kind == "wqT":
                pe.wait_ge(loaded["wq"], 16)
                for blk in range(MC):
                    for m in range(MC):
                        last = pe.transpose(b[:, blk * C + m * P:blk * C + (m + 1) * P], wq_raw[:, m, col(blk)], ident[:, :])
            elif kind == "mean":
                pe.wait_ge(scaled, 5)
                for m in range(MC):
                    last = pe.matmul(b[:, 0:C], mean_w[:, :], wog[:, m, :], start=m == 0, stop=m == MC - 1)
            elif kind == "bprime":
                for m in range(MC):
                    last = pe.matmul(b[:, 0:C], lnb_bc[:, m, :], wo_raw[:, m, :], start=m == 0, stop=m == MC - 1)
            elif kind == "ctxT":
                pe.wait_ge(loaded["ctx"], 16)
                for i in range(4):
                    last = pe.transpose(b[:, col(i)], ctx_raw[:, 4 * it[2] + i, col(it[1])], ident[:, :])
            elif kind == "wkvT":
                pe.wait_ge(loaded["wkv"], 16)
                for i in range(4):
                    last = pe.transpose(b[:, col(i)], wkv_raw[:, 4 * it[2] + i, col(it[1])], ident[:, :])
            elif kind == "wox":
                pe.wait_ge(loaded["wout"], 16)
                for r in range(2):
                    for m in range(MC):
                        last = pe.transpose(b[:, r * C + m * P:r * C + (m + 1) * P],
                                            wout_raw[:, m, col(2 * it[1] + r)], ident[:, :])
            else:
                ch, h = it[1:]
                if ch == 0 and h == 0:
                    pe.wait_ge(taken, u)
                c = slice(h * W, (h + 1) * W)
                for m in range(MC):
                    last = three_passes(pe, b[:, :], (wkvT_hi[:, m, col(ch)], wkvT_lo[:, m, col(ch)]),
                                        (ctxT_hi[:, m, c], ctxT_lo[:, m, c]), m == 0, m == MC - 1)
            last.then_inc(made, 1)

    @block.vector
    def _(dve):
        dve.memset(ones[:, :], 1.0).then_inc(scaled, 1)
        dve.memset(mean_w[:, :], 1.0 / C).then_inc(scaled, 1)
        dve.memset(ones_bf[:, :], 1.0)
        dve.memset(f32(rows[:, :]), 0.0)
        dve.memset(f32(ones33[:, :]), 0.0).then_inc(masked, 1)
        dve.wait_ge(masked, 1)
        dve.memset(f32(ones33[0:1, :]), 1.0)
        dve.memset(f32(ones33[32:33, :]), 1.0)
        dve.wait_ge(loaded["wo"], 64)
        dve.wait_ge(scaled, 2)
        dve.tensor_scalar(wog[:, 0, :], wo_raw[:, 0, :], lng[:, 0:1], None, ALU.mult).then_inc(scaled, 1)
        dve.tensor_scalar(wog[:, 1, :], wo_raw[:, 1, :], lng[:, 1:2], None, ALU.mult).then_inc(scaled, 1)
        dve.tensor_scalar(lnb_bc[:, 0, :], ones[:, :], lnb[:, 0:1], None, ALU.mult)
        dve.tensor_scalar(lnb_bc[:, 1, :], ones[:, :], lnb[:, 1:2], None, ALU.mult).then_inc(scaled, 1)
        n = 0
        for u, it in enumerate(items):
            b = bank[u % 8]
            kind = it[0]
            if kind in SPLITS:
                hi, lo = dest(it)
                dve.wait_ge(hi_made, sum(x[0] in SPLITS for x in items[:u + 1]))
                dve.tensor_tensor(lo, b[:, :], f32(hi), ALU.subtract).then_inc(taken, 1)
                continue
            dve.wait_ge(made, u + 1)
            if kind == "wqT":
                dve.wait_ge(eyes, 1)
                for blk in range(MC):
                    for m in range(MC):
                        src = b[:, blk * C + m * P:blk * C + (m + 1) * P]
                        if blk == m:
                            last = dve.tensor_tensor(wqT[:, blk, col(m)], src, ident[:, :], ALU.add)
                        else:
                            last = dve.tensor_copy(wqT[:, blk, col(m)], src)
            elif kind == "mean":
                for m in range(MC):
                    last = dve.scalar_tensor_tensor(woc[:, m, :], b[:, 0:C], -1.0, wog[:, m, :], ALU.mult, ALU.add)
            elif kind == "bprime":
                last = dve.tensor_tensor(bprime[:, :], b[:, 0:C], bobc[:, :], ALU.add)
            else:
                if n >= RING:
                    dve.wait_ge(staged[n % RING], 16 * (n // RING))
                last = dve.tensor_scalar(stage[:, n % RING, :], b[:, :], d_head ** -0.5 if it[1] < PAIRS else 1.0,
                                         None, ALU.mult)
                n += 1
            last.then_inc(taken, 1)
        dve.wait_ge(split_hi, 1)
        dve.tensor_tensor(wqx_lo[:, :, :], wqx_raw[:, :, :], f32(wqx_hi[:, :, :]), ALU.subtract)
        dve.wait_ge(loaded["wv"], 32)
        dve.wait_ge(loaded["wk"], 32)
        for w in (wv, wk):
            for st in range(2):
                for m in range(MC):
                    dve.tensor_tensor(w[:, m, st, col(m)], w[:, m, st, col(m)], ident[:, :], ALU.add)
        dve.wait_ge(loaded["mask"], 16)
        dve.tensor_scalar(maskrow[:, :], maskraw[:, :], 1.0, 2.0 ** 127, ALU.subtract, ALU.mult).then_inc(masked, 1)
        dve.wait_ge(loaded["small"], 80)
        dve.tensor_scalar(bvsum[:, :, :], bvsum[:, :, :], float(S), None, ALU.mult)


def ffn(nc, t, k, x2_scr, out_rows, C, MC, E, FF, FC, CAP, GT, GROUPS):
    W = 512
    HALF = GT // 2
    acc = k.sb("acc", [P, GT, C])
    x2T_hi = k.sb("x2T_hi", [P, MC, CAP], F32R)
    x2T_lo = k.sb("x2T_lo", [P, MC, CAP], F32R)
    w1_raw = k.sb("w1_raw", [P, MC, FF])
    w2_raw = k.sb("w2_raw", [P, FC, C])
    w1_hi = k.sb("w1_hi", [P, 2, MC, FF], F32R)
    w1_lo = k.sb("w1_lo", [P, 2, MC, FF], F32R)
    w2_hi = k.sb("w2_hi", [P, 2, FC, C], F32R)
    w2_lo = k.sb("w2_lo", [P, 2, FC, C], F32R)
    hT_hi = k.sb("hT_hi", [P, 2, FC, W], F32R)
    hT_lo = k.sb("hT_lo", [P, 2, FC, W], F32R)
    ident = k.sb("ident_f", [P, P])
    ones = k.sb("ones_f", [P, P], BF16)
    tri = k.sb("tri", [P, P], BF16)
    rw = k.sb("rw", [P, MC, E])
    rw_hi = k.sb("rw_hi", [P, MC, E], F32R)
    rw_lo = k.sb("rw_lo", [P, MC, E], F32R)
    rb = k.sb("rb", [P, E])
    lg = k.sb("lg", [P, GT, E])
    lmax = k.sb("lmax", [P, GT])
    lsum = k.sb("lsum", [P, GT])
    lrec = k.sb("lrec", [P, GT])
    chosen = k.sb("chosen", [P, GT, E], BF16)
    rank = k.sb("rank", [P, GT, E])
    coef = k.sb("coef", [P, GT, E])
    taken_before = k.sb("taken_before", [P, E])
    fewest = k.sb("fewest", [P, 1])
    groups_f = k.sb("groups_f", [P, 1])
    groups_i = k.sb("groups_i", [P, 1], I32)
    half_exp = k.sb("half_exp", [P, HALF])
    bst = k.sb("bst_f", [P, GT, 6])
    mv = k.sb("mv_f", [P, GT, 2])
    ve = k.sb("ve_f", [P, GT])
    rstd = k.sb("rstd_f", [P, GT])
    nmr = k.sb("nmr_f", [P, GT])
    up = [k.ps(f"up{i}") for i in range(4)]
    dn = [k.ps(f"dn{i}") for i in range(2)]
    tr = [k.ps(f"trf{i}") for i in range(2)]
    s = {n: k.sem("f_" + n) for n in (
        "small_loaded", "zeroed", "eyes", "rw_hi_made", "rw_lo_made", "acc_loaded", "w1_loaded", "w2_loaded", "w_hi_made", "w_lo_made",
        "xt_made", "xt_hi", "xt_taken", "logits_made", "shifted", "exp_made", "chosen_made", "ranks_made",
        "route_step", "coef_made", "up_made", "up_hi", "up_free", "dn_made", "dn_free",
        "mv_made", "bst_made", "ve_made", "ve2_made", "rstd_made", "nmr_made", "out_ready", "out_stored")}
    STEPS = 12
    block = k.stack.enter_context(nc.Block())
    last_pair = E - 2
    counted = {}

    def groups_and_experts(eng, name, begin, expert, end):
        n_groups = eng.alloc_register(name)
        eng.reg_mov(n_groups, 1)
        with eng.Fori(0, n_groups) as g:
            begin(g)
            with eng.Fori(0, last_pair, 2) as e:
                for u in range(2):
                    expert(g, g * E + e + u, e + u, u)
            for e in (E - 2, E - 1):
                expert(g, g * E + e, e, e % 2)
            end(g)
            eng.reg_load(n_groups, groups_i[0:1, 0:1])

    @block.sync
    def _(sp):
        def load_weights(n, e):
            sp.wait_ge(s["w_lo_made"], 2 * n)
            pick = (lambda a: a[e]) if isinstance(e, int) else (lambda a: a[bass.ds(e, 1), :, :].rearrange("o a b -> (o a) b"))
            sp.dma_start(w1_raw[:, :, :], pick(t["L0_ffn_experts_inter"]).rearrange("(m p) f -> p m f", p=P)
                         ).then_inc(s["w1_loaded"], 16)
            sp.dma_start(w2_raw[:, :, :], pick(t["L0_ffn_experts_out"]).rearrange("(i p) c -> p i c", p=P)
                         ).then_inc(s["w2_loaded"], 16)

        def begin(g):
            sp.wait_ge(s["out_stored"], 32 * g)
            sp.dma_start(acc[:, :, :], x2_scr[bass.ds(g * CAP, CAP), :].rearrange("(i p) c -> p i c", p=P)
                         ).then_inc(s["acc_loaded"], 16)
            load_weights(g * E, 0)

        def expert(g, n, e, u):
            if not isinstance(e, int) or e < E - 1:
                load_weights(n + 1, e + 1)

        def end(g):
            for h in range(2):
                sp.wait_ge(s["out_ready"], g * GT + (h + 1) * HALF)
                sp.dma_start(out_rows[bass.ds(g * CAP + h * HALF * P, HALF * P), :].rearrange("(i p) c -> p i c", p=P),
                             acc[:, h * HALF:(h + 1) * HALF, :]).then_inc(s["out_stored"], 16)

        sp.dma_start(rb[:, :], t["L0_ffn_router_b"].unsqueeze(0).broadcast_to([P, E])).then_inc(s["small_loaded"], 16)
        with nc.allow_non_contiguous_dma(reason="eight rows"):
            for m in range(MC):
                sp.dma_start(rw[:, m, :], t["L0_ffn_router_w"][:, m * P:(m + 1) * P].rearrange("e p -> p e")
                             ).then_inc(s["small_loaded"], 16)
        groups_and_experts(sp, "groups_sp", begin, expert, end)
        sp.wait_ge(s["out_stored"], 32)

    @block.scalar
    def _(act):
        def split_weights(n, e, u, part):
            if part == 0:
                act.wait_ge(s["w1_loaded"], 16 * (n + 1))
                if not isinstance(e, int) or e >= 1:
                    act.wait_ge(s["dn_made"], GT * (n - 1))
            if part == 2:
                act.wait_ge(s["w2_loaded"], 16 * (n + 1))
            if part < 2:
                last = act.activation(w1_hi[:, u, part, :], w1_raw[:, part, :], ACT.Copy)
            else:
                c = slice((part - 2) * FC // 2, (part - 1) * FC // 2)
                last = act.activation(w2_hi[:, u, c, :], w2_raw[:, c, :], ACT.Copy)
            if part % 2:
                last.then_inc(s["w_hi_made"], 1)

        def begin(g):
            split_weights(g * E, 0, 0, 0)
            split_weights(g * E, 0, 0, 1)
            for i in range(4):
                act.wait_ge(s["xt_made"], 4 * g + i + 1)
                act.activation(x2T_hi[:, :, 2 * i * P:2 * (i + 1) * P].rearrange("p m (a u) -> p a m u", a=2),
                               tr[i % 2][:, :].rearrange("p (a m u) -> p a m u", a=2, m=MC), ACT.Copy
                               ).then_inc(s["xt_hi"], 1)
            split_weights(g * E, 0, 0, 2)
            split_weights(g * E, 0, 0, 3)
            act.wait_ge(s["shifted"], g + 1)
            act.activation(lg[:, :, :], lg[:, :, :], ACT.Exp).then_inc(s["exp_made"], 1)

        def expert(g, n, e, u):
            for h in range(2):
                for i in range(FC):
                    act.wait_ge(s["up_made"], 2 * FC * n + h * FC + i + 1)
                    act.activation(hT_hi[:, h, i, :], up[i % 4][:, :], ACT.Relu).then_inc(s["up_hi"], 1)
                    if i % 4 == 3 and (not isinstance(e, int) or e < E - 1):
                        split_weights(n + 1, e + 1, 1 - u, 2 * h + i // 4)

        def end(g):
            for h in range(2):
                act.wait_ge(s["nmr_made"], 2 * g + h + 1)
                for i in range(h * HALF, (h + 1) * HALF):
                    act.activation(acc[:, i, :], acc[:, i, :], ACT.Identity, bias=nmr[:, i:i + 1],
                                   scale=rstd[:, i:i + 1]).then_inc(s["out_ready"], 1)

        act.wait_ge(s["small_loaded"], 16 * (1 + MC))
        act.activation(rw_hi[:, :, :], rw[:, :, :], ACT.Copy).then_inc(s["rw_hi_made"], 1)
        groups_and_experts(act, "groups_act", begin, expert, end)

    @block.gpsimd
    def _(pool):
        def split_weights(n, u):
            for part, (raw, hi, lo) in enumerate(((w1_raw, w1_hi, w1_lo), (w2_raw, w2_hi, w2_lo))):
                pool.wait_ge(s["w_hi_made"], 2 * n + part + 1)
                pool.tensor_tensor(lo[:, u, :, :], raw[:, :, :], f32(hi[:, u, :, :]), ALU.subtract
                                   ).then_inc(s["w_lo_made"], 1)

        def begin(g):
            split_weights(g * E, 0)

        def expert(g, n, e, u):
            if not isinstance(e, int) or e < E - 1:
                split_weights(n + 1, 1 - u)

        def end(g):
            for h in range(2):
                c = slice(h * HALF, (h + 1) * HALF)
                counted["mv"].wait_next(g * GT + (h + 1) * HALF)
                pool.tensor_scalar(ve[:, c], mv[:, c, 1], EPS, None, ALU.add).then_inc(s["ve_made"], 1)
                pool.wait_ge(s["ve_made"], 2 * g + h + 1)
                pool.tensor_tensor(rstd[:, c], ve[:, c], half_exp[:, :], ALU.pow).then_inc(s["rstd_made"], 1)
                counted["rstd"].wait_next(2 * g + h + 1)
                pool.tensor_scalar(ve[:, c], mv[:, c, 0], -1.0, None, ALU.mult).then_inc(s["ve2_made"], 1)
                pool.wait_ge(s["ve2_made"], 2 * g + h + 1)
                pool.tensor_tensor(nmr[:, c], ve[:, c], rstd[:, c], ALU.mult).then_inc(s["nmr_made"], 1)

        pool.memset(ident[:, :], 0.0).then_inc(s["zeroed"], 1)
        pool.memset(tri[:, :], 1.0).then_inc(s["zeroed"], 1)
        pool.memset(half_exp[:, :], -0.5)
        pool.wait_ge(s["zeroed"], 2)
        pool.affine_select(out=ident[:, :], in_=ident[:, :], compare_op=ALU.not_equal, fill=1.0, base=0,
                           pattern=[[-1, P]], channel_multiplier=1).then_inc(s["eyes"], 1)
        pool.affine_select(out=tri[:, :], in_=tri[:, :], compare_op=ALU.is_ge, fill=0.0, base=0,
                           pattern=[[1, P]], channel_multiplier=-1).then_inc(s["eyes"], 1)
        counted["mv"] = Counted(pool, s["mv_made"], "count_mv", HALF)
        counted["rstd"] = Counted(pool, s["rstd_made"], "count_rstd")
        counted["mv"].enter_loop()
        counted["rstd"].enter_loop()
        groups_and_experts(pool, "groups_pool", begin, expert, end)

    @block.tensor
    def _(pe):
        def begin(g):
            pe.wait_ge(s["acc_loaded"], 16 * (g + 1))
            for i in range(4):
                if i >= 2:
                    pe.wait_ge(s["xt_taken"], 4 * g + i - 1)
                for a in range(2):
                    for m in range(MC):
                        o = (a * MC + m) * P
                        last = pe.transpose(tr[i % 2][:, o:o + P], acc[:, 2 * i + a, m * P:(m + 1) * P], ident[:, :])
                last.then_inc(s["xt_made"], 1)
            pe.wait_ge(s["xt_taken"], 4 * g + 4)
            for i in range(GT):
                for m in range(MC):
                    c = slice(i * P, (i + 1) * P)
                    last = three_passes(pe, tr[0][:, i * E:(i + 1) * E], (x2T_hi[:, m, c], x2T_lo[:, m, c]),
                                        (rw_hi[:, m, :], rw_lo[:, m, :]), m == 0, m == MC - 1)
            last.then_inc(s["logits_made"], 1)
            pe.wait_ge(s["chosen_made"], g + 1)
            for i in range(GT + 1):
                o = i * E
                if i < GT:
                    last = pe.matmul(tr[1][:, o:o + E], tri[:, :], chosen[:, i, :], start=True, stop=i == 0)
                for b in range(i):
                    last = pe.matmul(tr[1][:, o:o + E], ones[:, :], chosen[:, b, :], start=(i == GT and b == 0),
                                     stop=b == i - 1)
            last.then_inc(s["ranks_made"], 1)

        def expert(g, n, e, u):
            for h in range(2):
                if h == 0:
                    pe.wait_ge(s["w_lo_made"], 2 * n + 1)
                c = slice(h * W, (h + 1) * W)
                for i in range(FC):
                    pe.wait_ge(s["up_free"], 2 * FC * n + h * FC + i + 1)
                    f = slice(i * P, (i + 1) * P)
                    for m in range(MC):
                        last = three_passes(pe, up[i % 4][:, :], (w1_hi[:, u, m, f], w1_lo[:, u, m, f]),
                                            (x2T_hi[:, m, c], x2T_lo[:, m, c]), m == 0, m == MC - 1)
                    last.then_inc(s["up_made"], 1)
            pe.wait_ge(s["w_lo_made"], 2 * n + 2)
            for i in range(GT):
                h, r = i // HALF, slice(i % HALF * P, (i % HALF + 1) * P)
                if i % HALF == 0:
                    pe.wait_ge(s["up_free"], 4 + 2 * FC * n + (h + 1) * FC)
                pe.wait_ge(s["dn_free"], GT * n + i + 1)
                for f in range(FC):
                    last = three_passes(pe, dn[i % 2][:, 0:C], (hT_hi[:, h, f, r], hT_lo[:, h, f, r]),
                                        (w2_hi[:, u, f, :], w2_lo[:, u, f, :]), f == 0, f == FC - 1)
                last.then_inc(s["dn_made"], 1)

        pe.wait_ge(s["eyes"], 2)
        pe.wait_ge(s["rw_lo_made"], 1)
        groups_and_experts(pe, "groups_pe", begin, expert, lambda g: None)

    @block.vector
    def _(dve):
        def begin(g):
            step = [0]

            def then(ins, *done):
                step[0] += 1
                ins.then_inc(s["route_step"], 1)
                dve.wait_ge(s["route_step"], g * STEPS + step[0])

            for i in range(4):
                dve.wait_ge(s["xt_hi"], 4 * g + i + 1)
                c = slice(2 * i * P, 2 * (i + 1) * P)
                dve.tensor_tensor(x2T_lo[:, :, c].rearrange("p m (a u) -> p a m u", a=2),
                                  tr[i % 2][:, :].rearrange("p (a m u) -> p a m u", a=2, m=MC),
                                  f32(x2T_hi[:, :, c]).rearrange("p m (a u) -> p a m u", a=2),
                                  ALU.subtract).then_inc(s["xt_taken"], 1)
            grid = lambda ap: ap.rearrange("p (i e) -> p i e", e=E)
            over_experts = lambda ap: ap.unsqueeze(2).broadcast_to([P, GT, E])
            over_tiles = lambda ap: ap.unsqueeze(1).broadcast_to([P, GT, E])
            dve.wait_ge(s["logits_made"], g + 1)
            then(dve.tensor_tensor(lg[:, :, :], grid(tr[0][:, 0:GT * E]), over_tiles(rb[:, :]), ALU.add))
            then(dve.tensor_reduce(lmax[:, :], lg[:, :, :], AX.X, ALU.max))
            dve.tensor_tensor(lg[:, :, :], lg[:, :, :], over_experts(lmax[:, :]), ALU.subtract).then_inc(s["shifted"], 1)
            dve.wait_ge(s["exp_made"], g + 1)
            then(dve.tensor_reduce(lsum[:, :], lg[:, :, :], AX.X, ALU.add))
            then(dve.reciprocal(lrec[:, :], lsum[:, :]))
            then(dve.tensor_tensor(lg[:, :, :], lg[:, :, :], over_experts(lrec[:, :]), ALU.mult))
            dve.tensor_scalar(chosen[:, :, :], lg[:, :, :], 0.0, None, ALU.is_gt).then_inc(s["chosen_made"], 1)
            dve.wait_ge(s["ranks_made"], g + 1)
            then(dve.tensor_tensor(rank[:, :, :], grid(tr[1][:, 0:GT * E]), over_tiles(taken_before[:, :]), ALU.add))
            then(dve.tensor_tensor(taken_before[:, :], taken_before[:, :], tr[1][:, GT * E:(GT + 1) * E], ALU.add))
            then(dve.tensor_scalar(rank[:, :, :], rank[:, :, :], float(CAP), None, ALU.is_le))
            then(dve.tensor_tensor(coef[:, :, :], rank[:, :, :], lg[:, :, :], ALU.mult))
            then(dve.tensor_reduce(fewest[:, :], taken_before[:, :], AX.X, ALU.min))
            then(dve.tensor_scalar(groups_f[:, :], fewest[:, :], float(CAP), float(GROUPS - 1), ALU.is_lt, ALU.mult))
            dve.wait_ge(s["w_lo_made"], 2 * E * g + 1)
            dve.tensor_scalar(groups_i[:, :], groups_f[:, :], 1.0, None, ALU.add).then_inc(s["route_step"], 1)

        def expert(g, n, e, u):
            for h in range(2):
                for i in range(FC):
                    dve.wait_ge(s["up_hi"], 2 * FC * n + h * FC + i + 1)
                    dve.scalar_tensor_tensor(hT_lo[:, h, i, :], up[i % 4][:, :], 0.0, f32(hT_hi[:, h, i, :]),
                                             ALU.max, ALU.subtract).then_inc(s["up_free"], 1)
            for i in range(GT):
                dve.wait_ge(s["dn_made"], GT * n + i + 1)
                col = coef[:, i, e:e + 1] if isinstance(e, int) else coef[:, i, bass.ds(e, 1)]
                dve.scalar_tensor_tensor(acc[:, i, :], dn[i % 2][:, 0:C], col, acc[:, i, :],
                                         ALU.mult, ALU.add).then_inc(s["dn_free"], 1)

        def end(g):
            for i in range(GT):
                dve.wait_ge(s["dn_free"], GT * E * g + GT * (E - 1) + i + 1 + 2)
                dve.bn_stats(bst[:, i, :], acc[:, i, :]).then_inc(s["bst_made"], 1)
                counted["bst"].wait_next(GT * g + i + 1)
                dve.bn_aggr(mv[:, i, :], bst[:, i, :]).then_inc(s["mv_made"], 1)

        dve.memset(taken_before[:, :], 0.0).then_inc(s["up_free"], 4)
        dve.memset(ones[:, :], 1.0).then_inc(s["dn_free"], 2)
        dve.wait_ge(s["rw_hi_made"], 1)
        dve.wait_ge(s["dn_free"], 2)
        dve.tensor_tensor(rw_lo[:, :, :], rw[:, :, :], f32(rw_hi[:, :, :]), ALU.subtract).then_inc(s["rw_lo_made"], 1)
        counted["bst"] = Counted(dve, s["bst_made"], "count_bst")
        counted["bst"].enter_loop()
        groups_and_experts(dve, "groups_dve", begin, expert, end)


_INS = ["x", "ctx_1024", "mask_BxS2_bf1", "L0_attn_Wq", "L0_attn_bq", "L0_attn_Wk", "L0_attn_bk",
        "L0_attn_Wv", "L0_attn_bv", "L0_attn_Wo", "L0_attn_bo", "L0_attn_ln_g", "L0_attn_ln_b",
        "L0_xattn_Wq", "L0_xattn_Wkv", "L0_xattn_Wout", "L0_xattn_b_out",
        "L0_ffn_router_w", "L0_ffn_router_b", "L0_ffn_experts_inter", "L0_ffn_experts_out"]


def kernel(**inputs):
    import numpy as np
    import concourse.bacc as bacc
    from concourse.bass_utils import run_bass_kernel_spmd

    nc = bacc.Bacc("TRN2", target_bir_lowering=False, num_devices=1)
    arrays, aps = {}, {}
    for name in _INS:
        a = np.ascontiguousarray(inputs[name])
        arrays[f"in_{name}"] = a
        aps[name] = nc.dram_tensor(f"in_{name}", a.shape, mybir.dt.from_np(a.dtype), kind="ExternalInput").ap()
    shape = arrays["in_x"].shape
    aps["out"] = nc.dram_tensor("out_x", shape, F32, kind="ExternalOutput").ap()
    build(nc, aps)
    r = run_bass_kernel_spmd(nc, [arrays], core_ids=[0])
    return r.results[0]["out_x"]
```

```python
from contextlib import ExitStack

import concourse.bass as bass
from concourse import mybir
from concourse.alu_op_type import AluOpType as ALU

ACT = mybir.ActivationFunctionType
AX = mybir.AxisListType
F32 = mybir.dt.float32
F32R = mybir.dt.float32r
BF16 = mybir.dt.bfloat16
I32 = mybir.dt.int32

P = 128
EPS = 1e-5
SMALLEST = 2.0 ** -126


def f32(ap):
    return ap.bitcast(F32)


def build(nc, t):
    NB, S, C = t["x"].shape
    NKV = t["ctx_1024"].shape[1]
    INNER = t["L0_xattn_Wq"].shape[0]
    E, _, FF = t["L0_ffn_experts_inter"].shape
    MC = C // P
    TPB = S // P
    PAIRS = INNER // P
    KEYS = 2 * PAIRS * NKV
    HEADS = 2 * PAIRS
    assert (MC, TPB, PAIRS, NKV) == (2, 4, 8, 64)
    TOK = NB * S
    CAP = TOK // E
    GT_ = CAP // P
    GROUPS = TOK // CAP
    FC = FF // P

    kv_scr = nc.dram_tensor("kv_scratch", (2, NB, P, PAIRS, NKV), F32).ap()
    x2_scr = nc.dram_tensor("x2_scratch", (TOK, C), F32).ap()
    out_rows = t["out"].rearrange("b s c -> (b s) c")

    with ExitStack() as whole:
        k = Names(nc, whole)
        first = FirstLoads(k.sb("acc", [P, GT_, C]), k.sb("w1_raw", [P, MC, FF]), k.sb("w2_raw", [P, FC, C]),
                           k.sem("f_acc_loaded"), k.sem("f_w1_loaded"), k.sem("f_w2_loaded"))
        with ExitStack() as phase:
            setup_and_attention(nc, t, Names(nc, phase), first, kv_scr, x2_scr, out_rows,
                                NB, S, C, NKV, MC, TPB, PAIRS, KEYS, HEADS, CAP)
        with ExitStack() as phase:
            ffn(nc, t, Names(nc, phase), first, x2_scr, out_rows, C, MC, E, FF, FC, CAP, GT_, GROUPS)


class FirstLoads:

    def __init__(self, acc, w1_raw, w2_raw, acc_loaded, w1_loaded, w2_loaded):
        self.acc, self.w1_raw, self.w2_raw = acc, w1_raw, w2_raw
        self.acc_loaded, self.w1_loaded, self.w2_loaded = acc_loaded, w1_loaded, w2_loaded

    def load_x2(self, sp, rows):
        sp.dma_start(self.acc[:, :, :], rows.rearrange("(i p) c -> p i c", p=P)).then_inc(self.acc_loaded, 16)

    def load_weights(self, sp, t, e):
        if isinstance(e, int):
            w1, w2 = t["L0_ffn_experts_inter"][e], t["L0_ffn_experts_out"][e]
        else:
            w1, w2 = (t[n][bass.ds(e, 1), :, :].rearrange("o a b -> (o a) b")
                      for n in ("L0_ffn_experts_inter", "L0_ffn_experts_out"))
        sp.dma_start(self.w1_raw[:, :, :], w1.rearrange("(m p) f -> p m f", p=P)).then_inc(self.w1_loaded, 16)
        sp.dma_start(self.w2_raw[:, :, :], w2.rearrange("(i p) c -> p i c", p=P)).then_inc(self.w2_loaded, 16)


class Names:

    def __init__(self, nc, stack):
        self.nc, self.stack = nc, stack

    def sb(self, name, shape, dt=F32):
        return self.stack.enter_context(self.nc.sbuf_tensor(name, shape, dt))

    def ps(self, name, shape=(P, 512), dt=F32):
        return self.stack.enter_context(self.nc.psum_tensor(name, list(shape), dt))

    def sem(self, name):
        return self.stack.enter_context(self.nc.semaphore(name))


class Counted:

    def __init__(self, eng, sem, name, step=1):
        self.eng, self.sem, self.step = eng, sem, step
        self.value = eng.alloc_register(name)
        self.last = 0

    def enter_loop(self):
        self.eng.reg_mov(self.value, self.last + self.step)

    def wait_next(self, value):
        if isinstance(value, int):
            self.eng.wait_ge(self.sem, value)
            self.last = value
        else:
            self.eng.wait_ge(self.sem, self.value)
            self.eng.reg_add(self.value, self.value, self.step)


def three_passes(pe, out, lhs, rhs, first, last):
    (lh, ll), (rh, rl) = lhs, rhs
    pe.matmul(out, lh, rh, start=first, stop=False)
    pe.matmul(out, lh, rl, start=False, stop=False)
    return pe.matmul(out, ll, rh, start=False, stop=last)


def setup_and_attention(nc, t, k, first, kv_scr, x2_scr, out_rows,
                        NB, S, C, NKV, MC, TPB, PAIRS, KEYS, HEADS, CAP):
    HK = KEYS // 2
    wv = k.sb("wv", [P, MC, 2, C])
    wk = k.sb("wk", [P, MC, 2, C])
    wqT = k.sb("wqT", [P, MC, C])
    woc = k.sb("woc", [P, MC, C])
    bvbc = k.sb("bvbc", [P, 2, C])
    bkbc = k.sb("bkbc", [P, 2, C])
    bprime = k.sb("bprime", [P, C])
    boutbc = k.sb("boutbc", [P, C])
    ident = k.sb("ident", [P, P])
    blockmask = k.sb("blockmask", [P, P])
    wqx = k.sb("wqx", [P, PAIRS, C])
    wox_hi = k.sb("wox_hi", [P, PAIRS, C], F32R)
    wox_lo = k.sb("wox_lo", [P, PAIRS, C], F32R)
    bq = k.sb("bq", [P, MC])
    bvsum = k.sb("bvsum", [P, 2, MC])
    maskrow = k.sb("maskrow", [1, NB * NKV], BF16)
    ones_bf = k.sb("ones_bf", [1, P], BF16)
    ones33 = k.sb("ones33", [33, P], F32R)
    epsc = k.sb("epsc", [P, 2])

    xraw = k.sb("xraw", [P, 2, TPB, C + 1])
    kraw = k.sb("kraw", [P, PAIRS, P])
    vraw = k.sb("vraw", [P, PAIRS, P])
    rows = k.sb("rows", [33, 2 * C], F32R)

    g_sb = k.sb("g_sb", [P, 2 * C + 2 - P])
    g10 = k.sb("g10", [P, P])
    t_sb = k.sb("t_sb", [P, MC, 2, C])
    r_sb = k.sb("r_sb", [P, 2, MC])
    r_sum = k.sb("r_sum", [P, 2 * MC])
    s_bc = k.sb("s_bc", [P, C])
    r_prod, wvT = first.acc[:, 0:2 * MC, :], first.acc[:, 2 * MC:4 * MC, :]
    s01 = k.sb("s01", [P, 2, MC, P])
    sprod = k.sb("sprod", [P, MC, P])
    sbdT = k.sb("sbdT", [P, MC, P])
    sbd = k.sb("sbd", [P, MC, P])
    sw = k.sb("sw", [P, MC, C])
    mmw_hi = k.sb("mmw_hi", [P, MC, 2 * C], F32R)
    mmw_lo = k.sb("mmw_lo", [P, MC, 2 * C], F32R)
    pws = [k.ps("pw0"), k.ps("pw1")]

    s = {n: k.sem(n) for n in (
        "x_loaded", "k_loaded", "v_loaded",
        "prep_made", "prep_hi", "prep_split", "prep_copied", "state_ready", "st_prod", "r_prod", "r_sum",
        "v_hi_made", "v_lo_made",
        "xT_made", "xT_hi", "xT_taken", "x1T_made", "x1T_hi", "x1T_taken", "xb_ready",
        "z_made", "z_taken", "x1_ready", "x1_biased",
        "sim_made", "max_made", "sim_taken", "exp_made", "sum_made", "rz_made", "p_ready",
        "pt_made", "pt_hi_made", "pt_taken", "o_made", "o_taken",
        "x2_ready", "out_ready", *(f"x2_stored{i}" for i in range(4)), *(f"out_stored{i}" for i in range(4)),
        "bst0", "bst1", "bst2", "bst3", "mv0", "mv1", "mv2", "mv3",
        "ve0", "ve1", "ve2", "ve3", "rstd0", "rstd1", "rstd2", "rstd3", "nmr1", "nmr2", "nmr3")}
    NTILES = NB * TPB

    ORDER = [("MW", 0, "a"), ("G", 0, "c"), ("B0", 0, "e"), ("GT", 0, "e"),
             ("B1", 1, "b"), ("B3", 1, "c"), ("B2", 1, "c"), ("T0", 1, "e"), ("T1", 1, "e"),
             ("R", 2, "c"), ("ST", 2, "e"),
             ("A0", 3, "a"), ("A1", 3, "a"), ("SW", 3, "b"), ("A2", 3, "b"), ("A3", 3, "c"), ("SB", 3, "d"),
             ("ROW", 3, "e"), ("M", 3, "e")]

    def batch_of(name, it):
        return it + (1 if name[0] == "A" or name == "MW" else 0 if name[0] == "B" else 2)

    def enabled(name, it):
        return not isinstance(it, int) or 0 <= batch_of(name, it) < NB

    NAMES = [n for n, _, _ in ORDER]
    COPIED = ("G", "GT", "R", "SW", "SB")
    SPLIT = ("A0", "A1", "A2", "A3", "B0", "B1", "B2", "B3", "M", "MW", "ROW")
    FINISHED = SPLIT + ("T0", "T1", "ST")

    def number(it, name, kinds=NAMES):
        names = [n for n in NAMES if n in kinds]
        if isinstance(it, int):
            return (sum(enabled(n, i) for i in range(-2, it) for n in names)
                    + sum(enabled(n, it) for n in names[:names.index(name) + 1]))
        before = sum(enabled(n, i) for i in range(-2, 0) for n in names)
        return it * len(names) + before + names.index(name) + 1

    def bank_of(name):
        return NAMES.index(name) % 2

    def prep_done(eng, it, name):
        if name in COPIED:
            need(eng, "prep_copied", number(it, name, COPIED))
        else:
            need(eng, "prep_split", number(it, name, FINISHED))

    def before_on_bank(it, name):
        i, back = NAMES.index(name) - 1, 0
        while not isinstance(it, int) or it - back >= -2:
            if i < 0:
                i, back = len(NAMES) - 1, back + 1
            if bank_of(NAMES[i]) == bank_of(name) and enabled(NAMES[i], it - back):
                return back, NAMES[i]
            i -= 1
        return 0, None

    OPERANDS = {"GT": ("G",), "T0": ("GT",), "T1": (), "R": (), "ST": (), "SW": (), "SB": (),
                "ROW": ("SW", "SB"), "M": ("SB",), "MW": ()}

    def at(slot, place, it):
        if isinstance(it, int) and it == -2:
            return []
        return [n for n, sl, pl in ORDER if (sl, pl) == (slot, place) and enabled(n, it)]

    def within(b):
        return not isinstance(b, int) or 0 <= b < NB

    def need(eng, name, value):
        if not isinstance(value, int) or value > 0:
            eng.wait_ge(s[name], value)

    counted = {}
    half = lambda buf, h: buf[:, :, h * HK:(h + 1) * HK]

    def sp_slot(sp, it, slot, e):
        if slot == 0 and within(it + 1):
            if within(it):
                need(sp, "prep_made", number(it - 1, "A3"))
            load_kv(sp, kraw, 0, it + 1, "k_loaded")
        if slot == 1 and within(it + 1):
            need(sp, "v_lo_made", it + 1)
            load_kv(sp, vraw, 1, it + 1, "v_loaded")
        if slot == 3 and within(it + 3):
            need(sp, "xT_made", 4 * (it + 2))
            need(sp, "xb_ready", 4 * (it + 2))
            need(sp, "x_loaded", 16 * (it + 3))
            sp.dma_start(xraw[:, (e + 1) % 2, :, 0:C], x_tiles(it + 3)).then_inc(s["x_loaded"], 16)
        n = 4 * it + slot
        if tile_exists(n - 3):
            store(sp, n - 3, (slot - 3) % 4, o_sb, "out_ready", "out_stored", out_rows)
        if tile_exists(n - 2):
            store(sp, n - 2, (slot - 2) % 4, x2, "x2_ready", "x2_stored", x2_scr)

    def tile_exists(n):
        return not isinstance(n, int) or 0 <= n < NTILES

    def store(sp, n, b, buf, ready, stored, dram):
        need(sp, ready, n + 1)
        rows_of = dram[n * P:(n + 1) * P, :] if isinstance(n, int) else dram[bass.ds(n * P, P), :]
        sp.dma_start(rows_of, buf[:, b, :]).then_inc(s[f"{stored}{b}"], 16)

    def x_tiles(b):
        if isinstance(b, int):
            return t["x"][b].rearrange("(i p) c -> p i c", p=P)
        return t["x"][bass.ds(b, 1), :, :].rearrange("o (i p) c -> p (o i) c", p=P)

    def load_kv(sp, dst, which, b, sem):
        for h in range(2):
            q = slice(64 * h, 64 * h + 64)
            if isinstance(b, int):
                src = kv_scr[which, b, q, :, :]
            else:
                src = kv_scr[which, bass.ds(b, 1), q, :, :].rearrange("o p r j -> (o p) r j")
            sp.dma_start(dst[q, :, 64 * h:64 * h + 64], src).then_inc(s[sem], 16)

    def pe_prep(pe, name, it, q):
        b = batch_of(name, it)
        pw = pws[bank_of(name)]
        latest = {}
        for back, other in [before_on_bank(it, name)] + [(0, x) for x in OPERANDS.get(name, ())]:
            if other:
                kind, place = other in COPIED, (-back, NAMES.index(other))
                latest[kind] = max(latest.get(kind, place), place)
        for back, i in latest.values():
            prep_done(pe, it + back, NAMES[i])
        i = int(name[-1]) if name[-1].isdigit() else 0
        if name == "G":
            need(pe, "x_loaded", 16 * (b + 1))
            for m, (lo_c, o) in enumerate(((0, 0), (P, C + 1))):
                for tile in range(TPB):
                    last = pe.matmul(pw[:, o:o + C + 1 - lo_c], xraw[:, q, tile, m * P:(m + 1) * P],
                                     xraw[:, q, tile, lo_c:C + 1], start=tile == 0, stop=tile == TPB - 1)
        elif name == "GT":
            last = pe.transpose(pw[:, 0:P], g_sb[:, P:C], ident[:, :])
        elif name[0] == "T":
            lhs = (g_sb[:, 0:P], g10[:, :]) if i == 0 else (g_sb[:, P:C], g_sb[:, C + 1:C + 1 + P])
            for m in range(MC):
                last = pe.matmul(pw[:, :], lhs[m], wv[:, m, :, :].rearrange("p s e -> p (s e)"),
                                 start=m == 0, stop=m == MC - 1)
        elif name == "R":
            for m in range(MC):
                col = C if m == 0 else C + 1 + P
                last = pe.matmul(pw[:, m * P:(m + 1) * P], g_sb[:, col:col + 1].broadcast_to([P, P]), ident[:, :],
                                 start=True, stop=True)
        elif name == "ST":
            for st in range(2):
                for blk in range(MC):
                    o = (st * MC + blk) * P
                    for m in range(MC):
                        last = pe.matmul(pw[:, o:o + P], t_sb[:, m, st, blk * P:(blk + 1) * P],
                                         wk[:, m, st, blk * P:(blk + 1) * P], start=m == 0, stop=m == MC - 1)
        elif name == "SW":
            need(pe, "state_ready", b + 1)
            for blk in range(MC):
                last = pe.matmul(pw[:, blk * C:(blk + 1) * C], sbdT[:, blk, :], woc[:, blk, :],
                                 start=True, stop=True)
        elif name == "SB":
            for blk in range(MC):
                last = pe.transpose(pw[:, blk * P:(blk + 1) * P], sbdT[:, blk, :], ident[:, :])
        elif name == "ROW":
            for blk in range(MC):
                pe.matmul(pw[0:1, blk * P:(blk + 1) * P], bq[:, blk:blk + 1], sbd[:, blk, :],
                          start=True, stop=True)
            for blk in range(MC):
                last = pe.matmul(pw[0:1, C:2 * C], bq[:, blk:blk + 1], sw[:, blk, :],
                                 start=blk == 0, stop=blk == MC - 1)
        elif name == "M":
            for m in range(MC):
                for blk in range(MC):
                    o = m * C + blk * P
                    last = pe.matmul(pw[:, o:o + P], wqT[:, blk, m * P:(m + 1) * P], sbd[:, blk, :],
                                     start=True, stop=True)
        elif name == "MW":
            for m in range(MC):
                for blk in range(MC):
                    last = pe.matmul(pw[:, m * C:(m + 1) * C], wqT[:, blk, m * P:(m + 1) * P], sw[:, blk, :],
                                     start=blk == 0, stop=blk == MC - 1)
        elif name[0] == "A":
            if i == 0:
                need(pe, "k_loaded", 32 * (b + 1))
            m, hf = i % 2, i // 2
            for r in range(PAIRS // 2):
                pr = hf * (PAIRS // 2) + r
                c = slice(m * P, (m + 1) * P)
                last = pe.matmul(pw[:, r * P:(r + 1) * P], wqx[:, pr, c], kraw[:, pr, :], start=True, stop=True)
        else:
            if i == 0:
                need(pe, "v_hi_made", b + 1)
                need(pe, "v_lo_made", b + 1)
            for r in range(2):
                pr = 2 * i + r
                last = three_passes(pe, pw[:, r * C:(r + 1) * C], (v_hi[:, pr, :], v_lo[:, pr, :]),
                                    (wox_hi[:, pr, :], wox_lo[:, pr, :]), True, True)
        last.then_inc(s["prep_made"], 1)

    def pe_x1T(pe, n, slot, q):
        if isinstance(n, int) and n > NTILES - 2:
            need(pe, "x1T_taken", n)
        need(pe, "xT_taken", min(n + 2, NTILES) if isinstance(n, int) else n + 2)
        need(pe, "x1_ready", n + 1)
        for m in range(MC):
            last = pe.transpose(x1t_bank[:, m * P:(m + 1) * P], x1[:, q, slot, m * P:(m + 1) * P], ident[:, :])
        last.then_inc(s["x1T_made"], 1)

    def pe_xT(pe, n, b, slot, q):
        need(pe, "x1T_taken", n - 1)
        if isinstance(n, int) and n < 2:
            need(pe, "xT_taken", n)
        need(pe, "x_loaded", 16 * (b + 1))
        for m in range(MC):
            last = pe.transpose(xt_bank[:, m * P:(m + 1) * P], xraw[:, q, slot, m * P:(m + 1) * P], ident[:, :])
        last.then_inc(s["xT_made"], 1)

    def pe_sim(pe, it, slot, h):
        n = 4 * it + slot
        need(pe, "sim_taken", 2 * n + h - 1)
        if h == 0:
            need(pe, "x1T_taken", n + 1)
            if slot == 0:
                prep_done(pe, it - 1, "A3")
        for m in range(MC):
            three_passes(pe, sim[h][:, :], (x1T_hi[:, slot, m, :], x1T_lo[:, slot, m, :]),
                         (half(a_hi, h)[:, m, :], half(a_lo, h)[:, m, :]), m == 0, False)
        row = maskrow[0:1, it * NKV:(it + 1) * NKV] if isinstance(it, int) else maskrow[0:1, bass.ds(it * NKV, NKV)]
        last = pe.matmul(sim[h][:, :].rearrange("p (g j) -> p g j", j=NKV), ones_bf[:, :],
                         row.unsqueeze(1).broadcast_to([1, HEADS // 2, NKV]), start=False, stop=True)
        last.then_inc(s["sim_made"], 1)

    def pe_pT(pe, n, par_n, h):
        need(pe, "p_ready", 2 * n + h + 1)
        need(pe, "pt_taken", 2 * n + h)
        for r in range(PAIRS // 2):
            c = (h * (PAIRS // 2) + r) * P
            last = pe.transpose(pt[:, r * P:(r + 1) * P], prob[:, par_n, c:c + P], ident[:, :])
        last.then_inc(s["pt_made"], 1)

    def pe_pB(pe, n, it, slot, h):
        need(pe, "pt_taken", 2 * n + h + 1)
        if h == 0:
            need(pe, "o_taken", n)
        if slot == 0:
            prep_done(pe, it, "B1" if h == 0 else "B3")
        for r in range(PAIRS // 2):
            pr = h * (PAIRS // 2) + r
            last = three_passes(pe, ob[:, 0:C], (pT_hi[:, pr, :], pT_lo[:, pr, :]),
                                (b_hi[:, pr, :], b_lo[:, pr, :]), pr == 0, pr == PAIRS - 1)
        if h == 1:
            last.then_inc(s["o_made"], 1)

    def pe_z(pe, it, slot):
        n = 4 * (it + 1) + slot
        need(pe, "z_taken", n)
        need(pe, "xT_taken", n + 1)
        if slot == 0:
            prep_done(pe, it, "MW")
        for m in range(MC):
            three_passes(pe, zb[:, :], (xT_hi[:, slot % 2, m, :], xT_lo[:, slot % 2, m, :]),
                         (mmw_hi[:, m, :], mmw_lo[:, m, :]), m == 0, False)
        pe.matmul(zb[:, :], ones33[:, :], rows[:, :], start=False, stop=True).then_inc(s["z_made"], 1)

    def parts(it, slot):
        n = 4 * it + slot
        isint = isinstance(it, int)
        has_sim = not isint or 0 <= it < NB
        has_z = not isint or 0 <= it + 1 < NB
        has_prev = not isint or 1 <= n <= NTILES
        has_xT = not isint or 0 <= n + 5 < NTILES
        has_x1T = not isint or 0 <= n + 3 < NTILES
        return has_sim, has_z, has_prev, has_xT, has_x1T

    def pe_slot(pe, it, slot, e):
        par = lambda a: (e + a) % 2
        has_sim, has_z, has_prev, has_xT, has_x1T = parts(it, slot)
        n = 4 * it + slot
        prep = lambda place: [pe_prep(pe, x, it, par(0)) for x in at(slot, place, it)]
        if has_sim:
            pe_sim(pe, it, slot, 0)
        prep("a")
        if has_sim:
            pe_sim(pe, it, slot, 1)
        if has_x1T:
            pe_x1T(pe, n + 3, (slot - 1) % 4, par(1 if slot else 0))
        prep("b")
        if has_prev:
            pe_pT(pe, n - 1, (slot - 1) % 2, 0)
        if has_z:
            pe_z(pe, it, slot)
        prep("c")
        if has_prev:
            pe_pT(pe, n - 1, (slot - 1) % 2, 1)
        if has_xT:
            pe_xT(pe, n + 5, it + 1 if slot < 3 else it + 2, (slot + 1) % 4, par(1 if slot < 3 else 2))
        prep("d")
        if has_prev:
            pe_pB(pe, n - 1, it if slot else it - 1, (slot - 1) % 4, 0)
        prep("e")
        if has_prev:
            pe_pB(pe, n - 1, it if slot else it - 1, (slot - 1) % 4, 1)
        prep("f")

    def prep_views(name):
        pw = pws[bank_of(name)]
        i = int(name[-1]) if name[-1].isdigit() else 0
        by_m = lambda buf: buf.rearrange("p (m e) -> p m e", m=MC)
        if name == "G":
            return pw[:, 0:2 * C + 2 - P], g_sb[:, :], None
        if name == "GT":
            return pw[:, 0:P], g10[:, :], None
        if name == "R":
            return pw[:, 0:C], s_bc[:, :], None
        if name == "SW":
            return by_m(pw[:, :]), sw[:, :, :], None
        if name == "SB":
            return by_m(pw[:, 0:MC * P]), sbd[:, :, :], None
        if name == "ROW":
            return pw[0:1, :], rows[0:1, :], rows[32:33, :]
        if name == "M":
            return by_m(pw[:, :]), mmw_hi[:, :, 0:C], mmw_lo[:, :, 0:C]
        if name == "MW":
            return by_m(pw[:, :]), mmw_hi[:, :, C:2 * C], mmw_lo[:, :, C:2 * C]
        if name[0] == "A":
            return pw[:, :], half(a_hi, i // 2)[:, i % 2, :], half(a_lo, i // 2)[:, i % 2, :]
        return (pw[:, :].rearrange("p (r c) -> p r c", r=2), b_hi[:, 2 * i:2 * i + 2, :],
                b_lo[:, 2 * i:2 * i + 2, :])

    def act_prep(act, name, it):
        if name in COPIED + SPLIT:
            src, dst, _ = prep_views(name)
            need(act, "prep_made", number(it, name))
            act.activation(dst, src, ACT.Copy).then_inc(s["prep_hi" if name in SPLIT else "prep_copied"], 1)

    def act_norm(act, ln, q, src, dst, done):
        act.activation(dst, src, ACT.Identity, bias=nmr[:, ln, q:q + 1], scale=rstd[:, ln, q:q + 1]).then_inc(s[done], 1)

    STATE_SLOT = 2

    def act_slot(act, it, slot, e):
        par = lambda a: (e + a) % 2
        has_sim, has_z, has_prev, has_xT, has_x1T = parts(it, slot)
        n = 4 * it + slot
        q = slot % 2
        prep = lambda place: [act_prep(act, x, it) for x in at(slot, place, it)]
        prep("a")
        if has_x1T:
            need(act, "nmr1", n + 4)
            need(act, "o_taken", n - 4)
            act_norm(act, 1, 1 - q, h1[:, 1 - q, :], x1[:, par(1 if slot else 0), (slot - 1) % 4, :], "x1_ready")
        if slot == 3 and within(it + 1):
            need(act, "v_loaded", 32 * (it + 2))
            if within(it):
                need(act, "prep_made", number(it, "B3"))
            act.activation(v_hi[:, :, :], vraw[:, :, :], ACT.Copy).then_inc(s["v_hi_made"], 1)
        if has_sim:
            act_exp(act, n, q, 0)
        if has_x1T:
            need(act, "x1T_made", n + 4)
            act.activation(x1T_hi[:, (slot - 1) % 4, :, :], x1t_bank.rearrange("p (m u) -> p m u", m=MC),
                           ACT.Copy).then_inc(s["x1T_hi"], 1)
        prep("b")
        if has_prev:
            act_pT(act, n - 1, 0)
        if has_sim:
            act_exp(act, n, q, 1)
        if tile_exists(n - 2):
            need(act, "nmr2", n - 1)
            act.wait_ge(s[f"x2_stored{(slot - 2) % 4}"], 16 * (it if slot >= 2 else it - 1) + 1)
            act_norm(act, 2, q, h2[:, q, :], x2[:, (slot - 2) % 4, :], "x2_ready")
        if tile_exists(n - 3):
            need(act, "nmr3", n - 2)
            act.wait_ge(s[f"out_stored{(slot - 3) % 4}"], 16 * (it if slot >= 3 else it - 1) + 1)
            act_norm(act, 3, 1 - q, x2[:, (slot - 3) % 4, :], o_sb[:, (slot - 3) % 4, :], "out_ready")
        prep("c")
        if has_prev:
            act_pT(act, n - 1, 1)
        if has_xT:
            need(act, "xT_made", n + 6)
            act.activation(xT_hi[:, (slot + 1) % 2, :, :], xt_bank.rearrange("p (m u) -> p m u", m=MC),
                           ACT.Copy).then_inc(s["xT_hi"], 1)
        prep("d")
        prep("e")
        prep("f")

    def act_exp(act, n, q, h):
        need(act, "sim_taken", 2 * n + h + 1)
        act.activation(prob[:, q, h * HK:(h + 1) * HK], prob[:, q, h * HK:(h + 1) * HK],
                       ACT.Exp).then_inc(s["exp_made"], 1)

    def act_pT(act, n, h):
        need(act, "pt_made", 2 * n + h + 1)
        act.activation(pT_hi[:, h * 4:h * 4 + 4, :], pt[:, :].rearrange("p (r u) -> p r u", u=P),
                       ACT.Copy).then_inc(s["pt_hi_made"], 1)

    def dve_prep(dve, name, it):
        n = number(it, name)
        pw = pws[bank_of(name)]
        if name in SPLIT:
            src, hi, lo = prep_views(name)
            need(dve, "prep_hi", number(it, name, SPLIT))
            dve.tensor_tensor(lo, src, f32(hi), ALU.subtract).then_inc(s["prep_split"], 1)
        elif name[0] == "T":
            m = int(name[1])
            need(dve, "prep_made", n)
            col = g_sb[:, C:C + 1] if m == 0 else g_sb[:, C + 1 + P:C + 2 + P]
            dve.scalar_tensor_tensor(t_sb[:, m, :, :].rearrange("p s e -> p (s e)"),
                                     bvbc[:, :, :].rearrange("p s e -> p (s e)"), col, pw[:, :],
                                     ALU.mult, ALU.add).then_inc(s["prep_split"], 1)
        elif name == "ST":
            b = batch_of(name, it)
            need(dve, "r_prod", b + 1)
            dve.tensor_reduce(r_sum[:, :], r_prod[:, :, :], AX.X, ALU.add).then_inc(s["r_sum"], 1)
            dve.wait_ge(s["r_sum"], 2 * b + 1)
            dve.tensor_tensor(r_sb[:, :, :].rearrange("p s b -> p (s b)"), r_sum[:, :],
                              bvsum[:, :, :].rearrange("p s b -> p (s b)"), ALU.add).then_inc(s["r_sum"], 1)
            dve.wait_ge(s["r_sum"], 2 * b + 2)
            need(dve, "prep_made", n)
            for st in range(2):
                for blk in range(MC):
                    o = (st * MC + blk) * P
                    last = dve.scalar_tensor_tensor(
                        s01[:, st, blk, :], bkbc[:, st, blk * P:(blk + 1) * P], r_sb[:, st, blk:blk + 1],
                        pw[:, o:o + P], ALU.mult, ALU.add)
            last.then_inc(s["prep_split"], 1)

    def dve_stats(dve, ln, n, q, src):
        need(dve, f"rstd{ln}", n - 1)
        if ln:
            need(dve, f"nmr{ln}", n - 1)
        dve.bn_stats(bst[:, ln, q, :], src).then_inc(s[f"bst{ln}"], 1)
        counted[f"bst{ln}"].wait_next(n + 1)
        dve.bn_aggr(mv[:, ln, q, :], bst[:, ln, q, :]).then_inc(s[f"mv{ln}"], 1)

    def dve_slot(dve, it, slot, e):
        par = lambda a: (e + a) % 2
        has_sim, has_z, has_prev, has_xT, has_x1T = parts(it, slot)
        n = 4 * it + slot
        q = slot % 2
        prep = lambda place: [dve_prep(dve, x, it) for x in at(slot, place, it)]
        if tile_exists(n - 2):
            need(dve, "o_made", n - 1)
            need(dve, "x1_biased", n - 1)
            need(dve, "x2_ready", n - 3)
            dve.tensor_tensor(h2[:, q, :], ob[:, 0:C], x1[:, par(0 if slot >= 2 else -1), (slot - 2) % 4, :],
                              ALU.add).then_inc(s["o_taken"], 1)
            dve.wait_ge(s["o_taken"], n - 1)
            dve_stats(dve, 2, n - 2, q, h2[:, q, :])
        if has_sim:
            dve_max(dve, n, 0)
        prep("a")
        if has_sim:
            dve_shift(dve, n, q, 0)
            dve_max(dve, n, 1)
            dve_shift(dve, n, q, 1)
        if has_x1T:
            need(dve, "x1T_hi", n + 4)
            d = (slot - 1) % 4
            dve.tensor_tensor(x1T_lo[:, d, :, :], x1t_bank.rearrange("p (m u) -> p m u", m=MC),
                              f32(x1T_hi[:, d, :, :]), ALU.subtract).then_inc(s["x1T_taken"], 1)
        prep("b")
        if has_prev:
            dve_pT(dve, n - 1, 0)
        if has_z:
            need(dve, "z_made", n + 5)
            dve_stats(dve, 0, n + 4, q, zb[:, 0:C])
        prep("c")
        if has_sim:
            need(dve, "exp_made", 2 * n + 2)
            dve.tensor_reduce(zsum[:, :], prob[:, q, :].rearrange("p (g j) -> p g j", j=NKV),
                              AX.X, ALU.add).then_inc(s["sum_made"], 1)
            dve.wait_ge(s["sum_made"], n + 1)
            need(dve, "p_ready", 2 * n - 2)
            dve.reciprocal(rz[:, q, :], zsum[:, :]).then_inc(s["rz_made"], 1)
        if has_prev:
            dve_pT(dve, n - 1, 1)
        if has_xT:
            need(dve, "xT_hi", n + 6)
            d = (slot + 1) % 2
            dve.tensor_tensor(xT_lo[:, d, :, :], xt_bank.rearrange("p (m u) -> p m u", m=MC),
                              f32(xT_hi[:, d, :, :]), ALU.subtract).then_inc(s["xT_taken"], 1)
        if has_z:
            need(dve, "rstd0", n + 5)
            need(dve, "xb_ready", n + 5)
            need(dve, "x1_ready", n + 3)
            dve.scalar_tensor_tensor(h1[:, q, :], zb[:, C:2 * C], rstd[:, 0, q:q + 1], xb[:, q, :],
                                     ALU.mult, ALU.add).then_inc(s["z_taken"], 1)
            dve.wait_ge(s["z_taken"], n + 5)
            dve_stats(dve, 1, n + 4, q, h1[:, q, :])
        prep("d")
        prep("e")
        if tile_exists(n - 2):
            need(dve, "x2_ready", n - 1)
            dve_stats(dve, 3, n - 2, q, x2[:, (slot - 2) % 4, :])
        prep("f")

    def by_head(ap):
        return ap.rearrange("p (g j) -> p g j", j=NKV)

    def dve_max(dve, n, h):
        need(dve, "sim_made", 2 * n + h + 1)
        dve.tensor_reduce(mx[:, h * 8:h * 8 + 8], by_head(sim[h][:, :]), AX.X, ALU.max).then_inc(s["max_made"], 1)

    def dve_shift(dve, n, q, h):
        dve.wait_ge(s["max_made"], 2 * n + h + 1)
        dve.tensor_tensor(by_head(prob[:, q, h * HK:(h + 1) * HK]), by_head(sim[h][:, :]),
                          mx[:, h * 8:h * 8 + 8].unsqueeze(2).broadcast_to([P, 8, NKV]),
                          ALU.subtract).then_inc(s["sim_taken"], 1)

    def dve_pT(dve, n, h):
        need(dve, "pt_hi_made", 2 * n + h + 1)
        dve.tensor_tensor(pT_lo[:, h * 4:h * 4 + 4, :], pt[:, :].rearrange("p (r u) -> p r u", u=P),
                          f32(pT_hi[:, h * 4:h * 4 + 4, :]), ALU.subtract).then_inc(s["pt_taken"], 1)

    def pool_rstd(pool, ln, n, q):
        counted[f"mv{ln}"].wait_next(n + 1)
        pool.tensor_scalar(ve[:, ln, q:q + 1], mv[:, ln, q, 1:2], EPS, None, ALU.add).then_inc(s[f"ve{ln}"], 1)
        pool.wait_ge(s[f"ve{ln}"], n + 1)
        need(pool, ("z_taken", "x1_ready", "x2_ready", "out_ready")[ln], n - 1)
        pool.tensor_tensor(rstd[:, ln, q:q + 1], ve[:, ln, q:q + 1], epsc[:, 0:1], ALU.pow).then_inc(s[f"rstd{ln}"], 1)
        if ln:
            counted[f"rstd{ln}"].wait_next(n + 1)
            pool.tensor_scalar(nmr[:, ln, q:q + 1], mv[:, ln, q, 0:1], rstd[:, ln, q:q + 1], -1.0,
                               ALU.mult, ALU.mult).then_inc(s[f"nmr{ln}"], 1)

    def pool_xb(pool, n, b, slot, q):
        need(pool, "x_loaded", 16 * (b + 1))
        need(pool, "z_taken", n - 1)
        pool.tensor_tensor(xb[:, slot % 2, :], xraw[:, q, slot, 0:C], bprime[:, :], ALU.add).then_inc(s["xb_ready"], 1)

    def pool_sums(pool, it):
        need(pool, "prep_copied", number(it, "R", COPIED))
        pool.tensor_tensor(r_prod[:, :, :], wvT[:, :, :], s_bc[:, :].unsqueeze(1).broadcast_to([P, 2 * MC, C]),
                           ALU.mult).then_inc(s["r_prod"], 1)

    def pool_state(pool, it):
        need(pool, "prep_split", number(it, "ST", FINISHED))
        pool.tensor_tensor(sprod[:, :, :], s01[:, 0, :, :], s01[:, 1, :, :], ALU.mult).then_inc(s["st_prod"], 1)
        pool.wait_ge(s["st_prod"], it + 3)
        pool.tensor_tensor(sbdT[:, :, :], sprod[:, :, :], blockmask[:, :].unsqueeze(1).broadcast_to([P, MC, P]),
                           ALU.mult).then_inc(s["state_ready"], 1)

    def pool_slot(pool, it, slot, e):
        par = lambda a: (e + a) % 2
        has_sim, has_z, has_prev, has_xT, has_x1T = parts(it, slot)
        n = 4 * it + slot
        q = slot % 2
        if tile_exists(n - 2):
            pool_rstd(pool, 2, n - 2, q)
        if slot == 3 and within(it + 1):
            need(pool, "v_hi_made", it + 2)
            pool.tensor_tensor(v_lo[:, :, :], vraw[:, :, :], f32(v_hi[:, :, :]), ALU.subtract).then_inc(s["v_lo_made"], 1)
        if has_x1T:
            need(pool, "x1T_made", n + 4)
            x1_tile = x1[:, par(1 if slot else 0), (slot - 1) % 4, :]
            pool.tensor_tensor(x1_tile, x1_tile, boutbc[:, :], ALU.add).then_inc(s["x1_biased"], 1)
        if has_z:
            pool_rstd(pool, 0, n + 4, q)
        if slot == STATE_SLOT and within(it + 2) and not (isinstance(it, int) and it == -2):
            pool_sums(pool, it)
        if has_xT:
            pool_xb(pool, n + 5, it + 1 if slot < 3 else it + 2, (slot + 1) % 4, par(1 if slot < 3 else 2))
        if has_sim:
            need(pool, "rz_made", n + 1)
            for h in range(2):
                part = by_head(prob[:, q, h * HK:(h + 1) * HK])
                pool.tensor_tensor(part, part, rz[:, q, h * 8:h * 8 + 8].unsqueeze(2).broadcast_to([P, 8, NKV]),
                                   ALU.mult).then_inc(s["p_ready"], 1)
        if slot == STATE_SLOT and within(it + 2) and not (isinstance(it, int) and it == -2):
            pool_state(pool, it)
        if has_z:
            pool_rstd(pool, 1, n + 4, q)
        if tile_exists(n - 2):
            pool_rstd(pool, 3, n - 2, q)

    FIRST_PREPS = [n for n in NAMES if enabled(n, -2)]

    def first_prep(eng, kind, i):
        name = FIRST_PREPS[i]
        if kind == "pe":
            pe_prep(eng, name, -2, 0)
        elif kind == "act":
            act_prep(eng, name, -2)
        elif kind == "dve":
            dve_prep(eng, name, -2)
        elif name == "R":
            pool_sums(eng, -2)
        elif name == "ST":
            pool_state(eng, -2)

    with ExitStack() as st:
        setup(nc, t, Names(nc, st), kv_scr, NB, S, C, NKV, MC, PAIRS,
              wv, wk, wqT, woc, bvbc, bkbc, bprime, boutbc, ident, blockmask,
              wqx, wox_hi, wox_lo, bq, bvsum, maskrow, ones_bf, ones33, epsc,
              xraw, kraw, vraw, rows, s["x_loaded"], wvT, len(FIRST_PREPS), first_prep)

    xT_hi = k.sb("xT_hi", [P, 2, MC, P], F32R)
    xT_lo = k.sb("xT_lo", [P, 2, MC, P], F32R)
    xb = k.sb("xb", [P, 2, C])
    x1 = k.sb("x1", [P, 2, TPB, C])
    x1T_hi = k.sb("x1T_hi", [P, TPB, MC, P], F32R)
    x1T_lo = k.sb("x1T_lo", [P, TPB, MC, P], F32R)
    a_hi = k.sb("a_hi", [P, MC, KEYS], F32R)
    a_lo = k.sb("a_lo", [P, MC, KEYS], F32R)
    b_hi = k.sb("b_hi", [P, PAIRS, C], F32R)
    b_lo = k.sb("b_lo", [P, PAIRS, C], F32R)
    v_hi = k.sb("v_hi", [P, PAIRS, P], F32R)
    v_lo = k.sb("v_lo", [P, PAIRS, P], F32R)
    prob = k.sb("prob", [P, 2, KEYS])
    mx = k.sb("mx", [P, HEADS])
    zsum = k.sb("zsum", [P, HEADS])
    rz = k.sb("rz", [P, 2, HEADS])
    pT_hi = k.sb("pT_hi", [P, PAIRS, P], F32R)
    pT_lo = k.sb("pT_lo", [P, PAIRS, P], F32R)
    h1 = k.sb("h1", [P, 2, C])
    h2 = k.sb("h2", [P, 2, C])
    x2 = k.sb("x2", [P, 4, C])
    o_sb = k.sb("o_sb", [P, 4, C])
    bst = k.sb("bst", [P, 4, 2, 6])
    mv = k.sb("mv", [P, 4, 2, 2])
    ve = k.sb("ve", [P, 4, 2])
    rstd = k.sb("rstd", [P, 4, 2])
    nmr = k.sb("nmr", [P, 4, 2])

    sim = [k.ps("sim0"), k.ps("sim1")]
    pt = k.ps("pt")
    zb = k.ps("zb")
    ob = k.ps("ob")
    tr = k.ps("tr")
    xt_bank, x1t_bank = tr[:, 0:C], tr[:, C:2 * C]
    block = k.stack.enter_context(nc.Block())

    FIRST, TRIPS = 2, (NB - 6) // 2

    def run(eng, slot_fn, late=lambda it: None):
        for it in range(-2, FIRST):
            for slot in range(0 if it > -2 else TPB - 1, TPB):
                slot_fn(eng, it, slot, it % 2)
        for c in counted.values():
            if c.eng is eng:
                c.enter_loop()
        with eng.Fori(0, TRIPS) as i:
            for u in range(2):
                for slot in range(TPB):
                    slot_fn(eng, 2 * i + (FIRST + u), slot, (FIRST + u) % 2)
        for it in range(FIRST + 2 * TRIPS, NB + 1):
            late(it)
            for slot in range(TPB if it < NB else 3):
                slot_fn(eng, it, slot, it % 2)

    @block.sync
    def _(sp):
        def group0(it):
            if it == NB - 2:
                sp.wait_ge(s["prep_split"], number(NB - 3, "ST", FINISHED))
                for i in range(4):
                    sp.wait_ge(s[f"x2_stored{i}"], 16 * CAP // (TPB * P) + 1)
                first.load_x2(sp, x2_scr[0:CAP, :])
                first.load_weights(sp, t, 0)

        run(sp, sp_slot, group0)
        for i in range(4):
            sp.wait_ge(s[f"x2_stored{i}"], 16 * NB + 1)
            sp.wait_ge(s[f"out_stored{i}"], 16 * NB + 1)

    @block.tensor
    def _(pe):
        run(pe, pe_slot)

    @block.scalar
    def _(act):
        run(act, act_slot)

    @block.vector
    def _(dve):
        for ln in range(4):
            counted[f"bst{ln}"] = Counted(dve, s[f"bst{ln}"], f"count_bst{ln}")
        run(dve, dve_slot)

    @block.gpsimd
    def _(pool):
        for ln in range(4):
            counted[f"mv{ln}"] = Counted(pool, s[f"mv{ln}"], f"count_mv{ln}")
            if ln:
                counted[f"rstd{ln}"] = Counted(pool, s[f"rstd{ln}"], f"count_rstd{ln}")
        for i in range(4):
            pool.memset(x2[:, i, 0:1], 0.0).then_inc(s[f"x2_stored{i}"], 1)
            pool.memset(o_sb[:, i, 0:1], 0.0).then_inc(s[f"out_stored{i}"], 1)
        run(pool, pool_slot)


def setup(nc, t, k, kv_scr, NB, S, C, NKV, MC, PAIRS, wv, wk, wqT, woc, bvbc, bkbc, bprime, boutbc, ident,
          blockmask, wqx, wox_hi, wox_lo, bq, bvsum, maskrow, ones_bf, ones33, epsc,
          xraw, kraw, vraw, rows, x_loaded, wvT, n_preps, first_prep):
    NCTX = NB * NKV
    CT = NCTX // P
    CH = 2 * PAIRS
    W = 512
    d_head = P // 2
    wq_raw = k.sb("wq_raw", [P, MC, C])
    wo_raw = k.sb("wo_raw", [P, MC, C])
    wog = k.sb("wog", [P, MC, C])
    wout_raw = k.sb("wout_raw", [P, MC, PAIRS * P])
    wkv_raw = k.sb("wkv_raw", [P, CH, C])
    ctx_raw = k.sb("ctx_raw", [P, CT, C])
    wkvT_hi = k.sb("wkvT_hi", [P, MC, CH * P], F32R)
    wkvT_lo = k.sb("wkvT_lo", [P, MC, CH * P], F32R)
    ctxT_hi = k.sb("ctxT_hi", [P, MC, NCTX], F32R)
    ctxT_lo = k.sb("ctxT_lo", [P, MC, NCTX], F32R)
    RING = 3
    stage = k.sb("stage", [P, RING, W])
    bobc = k.sb("bobc", [P, C])
    lng = k.sb("lng", [P, MC])
    lnb = k.sb("lnb", [P, MC])
    lnb_bc = k.sb("lnb_bc", [P, MC, P])
    ones = k.sb("ones", [P, P])
    mean_w = k.sb("mean_w", [P, P])
    maskraw = k.sb("maskraw", [1, NB * NKV], mybir.dt.uint8)
    BANKS = 6
    bank = [k.ps(f"su{i}") for i in range(BANKS)]
    names = ("wq", "wo", "wv", "wk", "small", "wout", "wqx", "mask")
    loaded = {n: k.sem(f"{n}_loaded") for n in names}
    made, hi_made, taken = k.sem("su_made"), k.sem("su_hi"), k.sem("su_taken")
    consts, scaled, eyes = k.sem("consts"), k.sem("scaled"), k.sem("eyes")
    wkv_loaded = [k.sem(f"wkv_loaded{g}") for g in range(CH // 4)]
    ctx_loaded = [k.sem(f"ctx_loaded{h}") for h in range(2)]
    masked, staged = k.sem("masked"), [k.sem(f"staged{i}") for i in range(RING)]
    mask_steps = k.sem("mask_steps")
    plus_eye, padded = k.sem("plus_eye"), k.sem("padded")

    items = [("ctxT", m, h) for h in range(NCTX // W) for m in range(MC)]
    for g in range(CH * P // W):
        items += [("wkvT", m, g) for m in range(MC)]
    items += [("wqT",), ("mean",), ("bprime",)]
    KV0 = len(items)
    items += [("kv", ch, h) for ch in range(CH) for h in range(NCTX // W)]
    items[KV0 + 4:KV0 + 4] = [("wvT", 0), ("wvT", 1)]
    items += [("wox", g) for g in range(PAIRS // 2)]

    def prep_after(u):
        i, rest = divmod(u - KV0 - 6, 3)
        return i if rest == 0 and 0 <= i < n_preps else None
    SPLITS = ("ctxT", "wkvT", "wox")
    col = lambda i: slice(i * P, (i + 1) * P)

    def dest(it):
        if it[0] == "ctxT":
            c = slice(it[2] * W, (it[2] + 1) * W)
            return ctxT_hi[:, it[1], c], ctxT_lo[:, it[1], c]
        if it[0] == "wkvT":
            c = slice(it[2] * W, (it[2] + 1) * W)
            return wkvT_hi[:, it[1], c], wkvT_lo[:, it[1], c]
        c = slice(2 * it[1], 2 * it[1] + 2)
        return (wox_hi[:, c, :].rearrange("p r c -> p (r c)"), wox_lo[:, c, :].rearrange("p r c -> p (r c)"))

    block = k.stack.enter_context(nc.Block())

    @block.sync
    def _(sp):
        flat = lambda ap: ap.rearrange("k c -> (k c)")
        rowbc = lambda ap, n: ap.unsqueeze(0).broadcast_to([P, n])
        ctx_tiles = t["ctx_1024"].rearrange("b j c -> (b j) c").rearrange("(i p) c -> p i c", p=P)
        for h in range(2):
            q = slice(h * CT // 2, (h + 1) * CT // 2)
            sp.dma_start(ctx_raw[:, q, :], ctx_tiles[:, q, :]).then_inc(ctx_loaded[h], 16)
        wkv_chunks = t["L0_xattn_Wkv"].rearrange("(i p) c -> p i c", p=P)
        for g in range(CH // 4):
            q = slice(4 * g, 4 * g + 4)
            sp.dma_start(wkv_raw[:, q, :], wkv_chunks[:, q, :]).then_inc(wkv_loaded[g], 16)
        sp.dma_start(wout_raw[:, :, :], t["L0_xattn_Wout"].rearrange("(m p) n -> p m n", p=P)).then_inc(loaded["wout"], 16)
        sp.dma_start(wqx[:, :, :], t["L0_xattn_Wq"].rearrange("(i p) c -> p i c", p=P)).then_inc(loaded["wqx"], 16)
        sp.dma_start(bvbc[:, :, :].rearrange("p s e -> p (s e)"), rowbc(flat(t["L0_attn_bv"]), 2 * C)).then_inc(loaded["small"], 16)
        sp.dma_start(bkbc[:, :, :].rearrange("p s e -> p (s e)"), rowbc(flat(t["L0_attn_bk"]), 2 * C)).then_inc(loaded["small"], 16)
        sp.dma_start(boutbc[:, :], rowbc(t["L0_xattn_b_out"], C)).then_inc(loaded["small"], 16)
        sp.dma_start(xraw[:, 0, :, 0:C], t["x"][0].rearrange("(i p) c -> p i c", p=P)).then_inc(x_loaded, 16)
        sp.dma_start(maskraw[:, :], t["mask_BxS2_bf1"].rearrange("b j -> (b j)").unsqueeze(0)).then_inc(loaded["mask"], 16)
        n = 0
        for u, it in enumerate(items):
            if it[0] == "kv":
                ch, h = it[1:]
                sp.wait_ge(taken, u + 1)
                nb = W // NKV
                sp.dma_start(kv_scr[ch // PAIRS, h * nb:(h + 1) * nb, :, ch % PAIRS, :].rearrange("b p j -> p b j"),
                             stage[:, n % RING, :].rearrange("p (b j) -> p b j", j=NKV)).then_inc(staged[n % RING], 16)
                n += 1
        for i in range(RING):
            sp.wait_ge(staged[i], 16 * ((n - i + RING - 1) // RING))

    @block.scalar
    def _(act):
        rowbc = lambda ap, n: ap.unsqueeze(0).broadcast_to([P, n])
        act.dma_start(wq_raw[:, :, :], t["L0_attn_Wq"].rearrange("(m p) d -> p m d", p=P)).then_inc(loaded["wq"], 16)
        act.dma_start(wo_raw[:, :, :], t["L0_attn_Wo"].rearrange("(m p) d -> p m d", p=P)).then_inc(loaded["wo"], 16)
        act.dma_start(bobc[:, :], rowbc(t["L0_attn_bo"], C)).then_inc(loaded["wo"], 16)
        with nc.allow_non_contiguous_dma(reason="a few hundred elements"):
            act.dma_start(lng[:, :], t["L0_attn_ln_g"].rearrange("(m p) -> p m", p=P)).then_inc(loaded["wo"], 16)
            act.dma_start(lnb[:, :], t["L0_attn_ln_b"].rearrange("(m p) -> p m", p=P)).then_inc(loaded["wo"], 16)
            act.dma_start(bq[:, :], t["L0_attn_bq"].rearrange("(m p) -> p m", p=P)).then_inc(loaded["small"], 16)
            act.dma_start(bvsum[:, :, :], t["L0_attn_bv"].rearrange("s (m p) -> p s m", p=P)).then_inc(loaded["small"], 16)
        for st in range(2):
            act.dma_start(wv[:, :, st, :], t["L0_attn_Wv"][st].rearrange("(m p) d -> p m d", p=P)).then_inc(loaded["wv"], 16)
            act.dma_start(wk[:, :, st, :], t["L0_attn_Wk"][st].rearrange("(m p) d -> p m d", p=P)).then_inc(loaded["wk"], 16)
        for u, it in enumerate(items):
            if it[0] in SPLITS:
                act.wait_ge(made, u + 1)
                act.activation(dest(it)[0], bank[u % BANKS][:, :], ACT.Copy).then_inc(hi_made, 1)
            if prep_after(u) is not None:
                first_prep(act, "act", prep_after(u))

    @block.gpsimd
    def _(pool):
        pool.memset(ident[:, :], 0.0).then_inc(consts, 1)
        pool.memset(blockmask[:, :], float((2.0 ** -10) ** 2)).then_inc(consts, 1)
        pool.wait_ge(consts, 2)
        pool.affine_select(out=ident[:, :], in_=ident[:, :], compare_op=ALU.not_equal, fill=1.0, base=0,
                           pattern=[[-1, P]], channel_multiplier=1).then_inc(eyes, 1)
        groups = blockmask[:, :].rearrange("p (h e) -> p h e", e=16)
        pool.affine_select(out=groups, in_=groups, compare_op=ALU.is_ge, fill=0.0, base=0,
                           pattern=[[-16, 8], [0, 16]], channel_multiplier=1).then_inc(mask_steps, 1)
        pool.wait_ge(mask_steps, 1)
        pool.affine_select(out=groups, in_=groups, compare_op=ALU.is_ge, fill=0.0, base=15,
                           pattern=[[16, 8], [0, 16]], channel_multiplier=-1).then_inc(mask_steps, 1)
        pool.memset(epsc[:, :], -0.5)
        pool.memset(kraw[:, :, :], 0.0)
        pool.memset(vraw[:, :, :], 0.0)
        for i in range(2):
            pool.memset(xraw[:, i, :, C:C + 1], 1.0).then_inc(padded, 1)
        for i in range(n_preps):
            first_prep(pool, "pool", i)

    @block.tensor
    def _(pe):
        pe.wait_ge(eyes, 1)
        for u, it in enumerate(items):
            b = bank[u % BANKS]
            if u >= BANKS:
                pe.wait_ge(taken, u - BANKS + 1)
            kind = it[0]
            if kind == "wqT":
                pe.wait_ge(loaded["wq"], 16)
                for blk in range(MC):
                    for m in range(MC):
                        last = pe.transpose(b[:, blk * C + m * P:blk * C + (m + 1) * P], wq_raw[:, m, col(blk)], ident[:, :])
            elif kind == "mean":
                pe.wait_ge(scaled, 5)
                for m in range(MC):
                    last = pe.matmul(b[:, 0:C], mean_w[:, :], wog[:, m, :], start=m == 0, stop=m == MC - 1)
            elif kind == "bprime":
                for m in range(MC):
                    last = pe.matmul(b[:, 0:C], lnb_bc[:, m, :], wo_raw[:, m, :], start=m == 0, stop=m == MC - 1)
            elif kind == "wvT":
                pe.wait_ge(plus_eye, 1)
                for blk in range(MC):
                    for m in range(MC):
                        last = pe.transpose(b[:, blk * C + m * P:blk * C + (m + 1) * P], wv[:, m, it[1], col(blk)], ident[:, :])
            elif kind == "ctxT":
                pe.wait_ge(ctx_loaded[it[2]], 16)
                for i in range(4):
                    last = pe.transpose(b[:, col(i)], ctx_raw[:, 4 * it[2] + i, col(it[1])], ident[:, :])
            elif kind == "wkvT":
                pe.wait_ge(wkv_loaded[it[2]], 16)
                for i in range(4):
                    last = pe.transpose(b[:, col(i)], wkv_raw[:, 4 * it[2] + i, col(it[1])], ident[:, :])
            elif kind == "wox":
                pe.wait_ge(loaded["wout"], 16)
                for r in range(2):
                    for m in range(MC):
                        last = pe.transpose(b[:, r * C + m * P:r * C + (m + 1) * P],
                                            wout_raw[:, m, col(2 * it[1] + r)], ident[:, :])
            else:
                ch, h = it[1:]
                if ch == 0 and h == 0:
                    pe.wait_ge(taken, u)
                c = slice(h * W, (h + 1) * W)
                for m in range(MC):
                    last = three_passes(pe, b[:, :], (wkvT_hi[:, m, col(ch)], wkvT_lo[:, m, col(ch)]),
                                        (ctxT_hi[:, m, c], ctxT_lo[:, m, c]), m == 0, m == MC - 1)
            last.then_inc(made, 1)
            if prep_after(u) is not None:
                if prep_after(u) == 0:
                    pe.wait_ge(padded, 2)
                first_prep(pe, "pe", prep_after(u))

    @block.vector
    def _(dve):
        dve.memset(ones[:, :], 1.0).then_inc(scaled, 1)
        dve.memset(mean_w[:, :], 1.0 / C).then_inc(scaled, 1)
        dve.memset(ones_bf[:, :], 1.0)
        dve.memset(f32(rows[:, :]), 0.0)
        dve.memset(f32(ones33[:, :]), 0.0).then_inc(masked, 1)
        dve.wait_ge(masked, 1)
        dve.memset(f32(ones33[0:1, :]), 1.0)
        dve.memset(f32(ones33[32:33, :]), 1.0)
        dve.wait_ge(loaded["wo"], 64)
        dve.wait_ge(scaled, 2)
        dve.tensor_scalar(wog[:, 0, :], wo_raw[:, 0, :], lng[:, 0:1], None, ALU.mult).then_inc(scaled, 1)
        dve.tensor_scalar(wog[:, 1, :], wo_raw[:, 1, :], lng[:, 1:2], None, ALU.mult).then_inc(scaled, 1)
        dve.tensor_scalar(lnb_bc[:, 0, :], ones[:, :], lnb[:, 0:1], None, ALU.mult)
        dve.tensor_scalar(lnb_bc[:, 1, :], ones[:, :], lnb[:, 1:2], None, ALU.mult).then_inc(scaled, 1)
        n = 0
        for u, it in enumerate(items):
            b = bank[u % BANKS]
            kind = it[0]
            if u == KV0 + 2:
                dve.wait_ge(loaded["wv"], 32)
                dve.wait_ge(loaded["wk"], 32)
                for w in (wv, wk):
                    for st in range(2):
                        for m in range(MC):
                            last = dve.tensor_tensor(w[:, m, st, col(m)], w[:, m, st, col(m)], ident[:, :], ALU.add)
                last.then_inc(plus_eye, 1)
                dve.wait_ge(loaded["small"], 80)
                dve.tensor_scalar(bvsum[:, :, :], bvsum[:, :, :], float(S), None, ALU.mult).then_inc(masked, 1)
                dve.wait_ge(masked, 2)
            if kind in SPLITS:
                hi, lo = dest(it)
                dve.wait_ge(hi_made, sum(x[0] in SPLITS for x in items[:u + 1]))
                dve.tensor_tensor(lo, b[:, :], f32(hi), ALU.subtract).then_inc(taken, 1)
                continue
            dve.wait_ge(made, u + 1)
            if kind == "wqT":
                dve.wait_ge(eyes, 1)
                for blk in range(MC):
                    for m in range(MC):
                        src = b[:, blk * C + m * P:blk * C + (m + 1) * P]
                        if blk == m:
                            last = dve.tensor_tensor(wqT[:, blk, col(m)], src, ident[:, :], ALU.add)
                        else:
                            last = dve.tensor_copy(wqT[:, blk, col(m)], src)
            elif kind == "wvT":
                last = dve.tensor_copy(wvT[:, MC * it[1]:MC * (it[1] + 1), :], b[:, :].rearrange("p (k c) -> p k c", c=C))
            elif kind == "mean":
                for m in range(MC):
                    last = dve.scalar_tensor_tensor(woc[:, m, :], b[:, 0:C], -1.0, wog[:, m, :], ALU.mult, ALU.add)
            elif kind == "bprime":
                last = dve.tensor_tensor(bprime[:, :], b[:, 0:C], bobc[:, :], ALU.add)
            else:
                if n >= RING:
                    dve.wait_ge(staged[n % RING], 16 * (n // RING))
                last = dve.tensor_scalar(stage[:, n % RING, :], b[:, :], d_head ** -0.5 if it[1] < PAIRS else 1.0,
                                         None, ALU.mult)
                n += 1
            last.then_inc(taken, 1)
            if prep_after(u) is not None:
                first_prep(dve, "dve", prep_after(u))
        dve.wait_ge(loaded["wqx"], 16)
        dve.wait_ge(loaded["mask"], 16)
        dve.tensor_scalar(maskrow[:, :], maskraw[:, :], 1.0, 2.0 ** 127, ALU.subtract, ALU.mult).then_inc(masked, 1)


def ffn(nc, t, k, first, x2_scr, out_rows, C, MC, E, FF, FC, CAP, GT, GROUPS):
    W = 512
    HALF = GT // 2
    PART = 2
    STORES = GT // PART
    acc = first.acc
    w1_raw, w2_raw = first.w1_raw, first.w2_raw
    x2T_hi = k.sb("x2T_hi", [P, MC, CAP], F32R)
    x2T_lo = k.sb("x2T_lo", [P, MC, CAP], F32R)
    w1_hi = k.sb("w1_hi", [P, 2, MC, FF], F32R)
    w1_lo = k.sb("w1_lo", [P, 2, MC, FF], F32R)
    w2_hi = k.sb("w2_hi", [P, 2, FC, C], F32R)
    w2_lo = k.sb("w2_lo", [P, 2, FC, C], F32R)
    hT_hi = k.sb("hT_hi", [P, 2, FC, W], F32R)
    hT_lo = k.sb("hT_lo", [P, 2, FC, W], F32R)
    ident = k.sb("ident_f", [P, P])
    ones = k.sb("ones_f", [P, P], BF16)
    tri = k.sb("tri", [P, P], BF16)
    rw = k.sb("rw", [P, MC, E])
    rw_hi = k.sb("rw_hi", [P, MC, E], F32R)
    rw_lo = k.sb("rw_lo", [P, MC, E], F32R)
    rb = k.sb("rb", [P, E])
    lgT = k.sb("lgT", [E, CAP])
    lg = k.sb("lg", [P, GT, E])
    lmax = k.sb("lmax", [P, GT])
    lsum = k.sb("lsum", [P, GT])
    lrec = k.sb("lrec", [P, GT])
    chosen = k.sb("chosen", [P, GT, E], BF16)
    rank = k.sb("rank", [P, GT, E])
    coef = k.sb("coef", [P, GT, E])
    taken_before = k.sb("taken_before", [P, E])
    fewest = k.sb("fewest", [P, 1])
    groups_f = k.sb("groups_f", [P, 1])
    groups_i = k.sb("groups_i", [P, 1], I32)
    half_exp = k.sb("half_exp", [P, PART])
    bst = k.sb("bst_f", [P, GT, 6])
    mv = k.sb("mv_f", [P, GT, 2])
    ve = k.sb("ve_f", [P, GT])
    rstd = k.sb("rstd_f", [P, GT])
    nmr = k.sb("nmr_f", [P, GT])
    up = [k.ps(f"up{i}") for i in range(4)]
    dn = [k.ps(f"dn{i}") for i in range(2)]
    tr = [k.ps(f"trf{i}") for i in range(2)]
    s = {n: k.sem("f_" + n) for n in (
        "small_loaded", "zeroed", "eyes", "rw_hi_made", "rw_lo_made", "w_hi_made", "w_lo_made",
        "xt_made", "xt_hi", "xt_taken", "lgT_made", "lgT_copied", "logits_made", "shifted", "exp_made", "chosen_made", "ranks_made",
        "route_step", "coef_made", "up_made", "up_hi", "up_free", "dn_made", "dn_free",
        "mv_made", "bst_made", "ve_made", "ve2_made", "rstd_made", "nmr_made", "out_ready", "out_stored")}
    s.update(acc_loaded=first.acc_loaded, w1_loaded=first.w1_loaded, w2_loaded=first.w2_loaded)
    STEPS = 12
    block = k.stack.enter_context(nc.Block())
    counted = {}

    def is_first(e):
        return isinstance(e, int) and e == 0

    def groups_and_experts(eng, name, begin, expert, end):
        n_groups = eng.alloc_register(name)
        eng.reg_mov(n_groups, 1)
        with eng.Fori(0, n_groups) as g:
            begin(g)
            expert(g, g * E, 0, 0)
            with eng.Fori(0, (E - 2) // 2) as j:
                for u in (1, 2):
                    expert(g, g * E + 2 * j + u, 2 * j + u, u % 2)
            expert(g, g * E + E - 1, E - 1, (E - 1) % 2)
            end(g)
            eng.reg_load(n_groups, groups_i[0:1, 0:1])

    @block.sync
    def _(sp):
        def load_weights(n, e):
            sp.wait_ge(s["w_lo_made"], 2 * n)
            first.load_weights(sp, t, e)

        def begin(g):
            with sp.If_ne(further, 0):
                sp.wait_ge(s["out_stored"], 16 * STORES * g)
                first.load_x2(sp, x2_scr[bass.ds(g * CAP, CAP), :])
                load_weights(g * E, 0)
            sp.reg_mov(further, 1)

        def expert(g, n, e, u):
            if not isinstance(e, int) or e < E - 1:
                load_weights(n + 1, e + 1)

        def end(g):
            for h in range(STORES):
                sp.wait_ge(s["out_ready"], g * GT + (h + 1) * PART)
                sp.dma_start(out_rows[bass.ds(g * CAP + h * PART * P, PART * P), :].rearrange("(i p) c -> p i c", p=P),
                             acc[:, h * PART:(h + 1) * PART, :]).then_inc(s["out_stored"], 16)
            sp.reg_add(stores, stores, 16 * STORES)

        sp.dma_start(rb[:, :], t["L0_ffn_router_b"].unsqueeze(0).broadcast_to([P, E])).then_inc(s["small_loaded"], 16)
        with nc.allow_non_contiguous_dma(reason="eight rows"):
            for m in range(MC):
                sp.dma_start(rw[:, m, :], t["L0_ffn_router_w"][:, m * P:(m + 1) * P].rearrange("e p -> p e")
                             ).then_inc(s["small_loaded"], 16)
        further = sp.alloc_register("further_groups")
        sp.reg_mov(further, 0)
        stores = sp.alloc_register("group_stores")
        sp.reg_mov(stores, 0)
        groups_and_experts(sp, "groups_sp", begin, expert, end)
        sp.wait_ge(s["out_stored"], 16 * STORES)
        sp.wait_ge(s["out_stored"], stores)

    @block.scalar
    def _(act):
        def split_weights(n, e, u, part):
            if part == 0:
                act.wait_ge(s["w1_loaded"], 16 * (n + 1))
                if not isinstance(e, int) or e >= 2:
                    act.wait_ge(s["dn_made"], GT * (n - 1))
                elif e == 1:
                    act.wait_ge(s["up_made"], 2 * FC * (n - 1) + 1)
            if part == 2:
                act.wait_ge(s["w2_loaded"], 16 * (n + 1))
            if part < 2:
                last = act.activation(w1_hi[:, u, part, :], w1_raw[:, part, :], ACT.Copy)
            else:
                c = slice((part - 2) * FC // 2, (part - 1) * FC // 2)
                last = act.activation(w2_hi[:, u, c, :], w2_raw[:, c, :], ACT.Copy)
            if part % 2:
                last.then_inc(s["w_hi_made"], 1)

        def begin(g):
            split_weights(g * E, 0, 0, 0)
            split_weights(g * E, 0, 0, 1)
            for i in range(4):
                act.wait_ge(s["xt_made"], 4 * g + i + 1)
                act.activation(x2T_hi[:, :, 2 * i * P:2 * (i + 1) * P].rearrange("p m (a u) -> p a m u", a=2),
                               tr[i % 2][:, :].rearrange("p (a m u) -> p a m u", a=2, m=MC), ACT.Copy
                               ).then_inc(s["xt_hi"], 1)
            split_weights(g * E, 0, 0, 2)
            split_weights(g * E, 0, 0, 3)

        def expert(g, n, e, u):
            for h in range(2):
                for i in range(FC):
                    act.wait_ge(s["up_made"], 2 * FC * n + h * FC + i + 1)
                    act.activation(hT_hi[:, h, i, :], up[i % 4][:, :], ACT.Relu).then_inc(s["up_hi"], 1)
                    if is_first(e) and (h, i) == (1, 1):
                        act.wait_ge(s["shifted"], g + 1)
                        act.activation(lg[:, :, :], lg[:, :, :], ACT.Exp).then_inc(s["exp_made"], 1)
                    if i % 4 == 3 and (not isinstance(e, int) or e < E - 1):
                        split_weights(n + 1, e + 1, 1 - u, 2 * h + i // 4)
                if h == 0 and is_first(e):
                    act.wait_ge(s["lgT_made"], g + 1)
                    act.activation(lgT[:, 0:W], tr[0][0:E, :], ACT.Copy)
                    act.activation(lgT[:, W:2 * W], tr[1][0:E, :], ACT.Copy).then_inc(s["lgT_copied"], 1)

        def end(g):
            for h in range(STORES):
                act.wait_ge(s["nmr_made"], STORES * g + h + 1)
                for i in range(h * PART, (h + 1) * PART):
                    act.activation(acc[:, i, :], acc[:, i, :], ACT.Identity, bias=nmr[:, i:i + 1],
                                   scale=rstd[:, i:i + 1]).then_inc(s["out_ready"], 1)

        act.wait_ge(s["small_loaded"], 16 * (1 + MC))
        act.activation(rw_hi[:, :, :], rw[:, :, :], ACT.Copy).then_inc(s["rw_hi_made"], 1)
        groups_and_experts(act, "groups_act", begin, expert, end)

    @block.gpsimd
    def _(pool):
        def split_weights(n, u):
            for part, (raw, hi, lo) in enumerate(((w1_raw, w1_hi, w1_lo), (w2_raw, w2_hi, w2_lo))):
                pool.wait_ge(s["w_hi_made"], 2 * n + part + 1)
                pool.tensor_tensor(lo[:, u, :, :], raw[:, :, :], f32(hi[:, u, :, :]), ALU.subtract
                                   ).then_inc(s["w_lo_made"], 1)

        def begin(g):
            split_weights(g * E, 0)

        def expert(g, n, e, u):
            if not isinstance(e, int) or e < E - 1:
                split_weights(n + 1, 1 - u)

        def end(g):
            for h in range(STORES):
                c = slice(h * PART, (h + 1) * PART)
                counted["mv"].wait_next(g * GT + (h + 1) * PART)
                pool.tensor_scalar(ve[:, c], mv[:, c, 1], EPS, None, ALU.add).then_inc(s["ve_made"], 1)
                pool.wait_ge(s["ve_made"], STORES * g + h + 1)
                pool.tensor_tensor(rstd[:, c], ve[:, c], half_exp[:, :], ALU.pow).then_inc(s["rstd_made"], 1)
                counted["rstd"].wait_next(STORES * g + h + 1)
                pool.tensor_scalar(ve[:, c], mv[:, c, 0], -1.0, None, ALU.mult).then_inc(s["ve2_made"], 1)
                pool.wait_ge(s["ve2_made"], STORES * g + h + 1)
                pool.tensor_tensor(nmr[:, c], ve[:, c], rstd[:, c], ALU.mult).then_inc(s["nmr_made"], 1)

        pool.memset(ident[:, :], 0.0).then_inc(s["zeroed"], 1)
        pool.memset(tri[:, :], 1.0).then_inc(s["zeroed"], 1)
        pool.memset(half_exp[:, :], -0.5)
        pool.wait_ge(s["zeroed"], 2)
        pool.affine_select(out=ident[:, :], in_=ident[:, :], compare_op=ALU.not_equal, fill=1.0, base=0,
                           pattern=[[-1, P]], channel_multiplier=1).then_inc(s["eyes"], 1)
        pool.affine_select(out=tri[:, :], in_=tri[:, :], compare_op=ALU.is_ge, fill=0.0, base=0,
                           pattern=[[1, P]], channel_multiplier=-1).then_inc(s["eyes"], 1)
        counted["mv"] = Counted(pool, s["mv_made"], "count_mv", PART)
        counted["rstd"] = Counted(pool, s["rstd_made"], "count_rstd")
        counted["mv"].enter_loop()
        counted["rstd"].enter_loop()
        groups_and_experts(pool, "groups_pool", begin, expert, end)

    @block.tensor
    def _(pe):
        def begin(g):
            pe.wait_ge(s["acc_loaded"], 16 * (g + 1))
            for i in range(4):
                if i >= 2:
                    pe.wait_ge(s["xt_taken"], 4 * g + i - 1)
                for a in range(2):
                    for m in range(MC):
                        o = (a * MC + m) * P
                        last = pe.transpose(tr[i % 2][:, o:o + P], acc[:, 2 * i + a, m * P:(m + 1) * P], ident[:, :])
                last.then_inc(s["xt_made"], 1)

        def logits(g):
            for h in range(2):
                c = slice(h * W, (h + 1) * W)
                for m in range(MC):
                    last = three_passes(pe, tr[h][0:E, :], (rw_hi[:, m, :], rw_lo[:, m, :]),
                                        (x2T_hi[:, m, c], x2T_lo[:, m, c]), m == 0, m == MC - 1)
            last.then_inc(s["lgT_made"], 1)

        def logits_back(g):
            for i in range(GT):
                last = pe.transpose(tr[0][:, i * E:(i + 1) * E], lgT[:, i * P:(i + 1) * P], ident[0:E, 0:E])
            last.then_inc(s["logits_made"], 1)

        def ranks(g):
            pe.wait_ge(s["chosen_made"], g + 1)
            for i in range(GT + 1):
                o = i * E
                if i < GT:
                    last = pe.matmul(tr[1][:, o:o + E], tri[:, :], chosen[:, i, :], start=True, stop=i == 0)
                for b in range(i):
                    last = pe.matmul(tr[1][:, o:o + E], ones[:, :], chosen[:, b, :], start=(i == GT and b == 0),
                                     stop=b == i - 1)
            last.then_inc(s["ranks_made"], 1)

        def expert(g, n, e, u):
            for h in range(2):
                if h == 0:
                    pe.wait_ge(s["w_lo_made"], 2 * n + 1)
                if is_first(e):
                    pe.wait_ge(s["xt_taken"], 4 * g + 2 * h + 2)
                c = slice(h * W, (h + 1) * W)
                for i in range(FC):
                    pe.wait_ge(s["up_free"], 2 * FC * n + h * FC + i + 1)
                    if is_first(e) and (h, i) == (1, 1):
                        pe.wait_ge(s["lgT_copied"], g + 1)
                    f = slice(i * P, (i + 1) * P)
                    for m in range(MC):
                        last = three_passes(pe, up[i % 4][:, :], (w1_hi[:, u, m, f], w1_lo[:, u, m, f]),
                                            (x2T_hi[:, m, c], x2T_lo[:, m, c]), m == 0, m == MC - 1)
                    last.then_inc(s["up_made"], 1)
                    if is_first(e) and (h, i) == (1, 1):
                        logits_back(g)
                if is_first(e):
                    (logits, ranks)[h](g)
            pe.wait_ge(s["w_lo_made"], 2 * n + 2)
            for i in range(GT):
                h, r = i // HALF, slice(i % HALF * P, (i % HALF + 1) * P)
                if i % HALF == 0:
                    pe.wait_ge(s["up_free"], 4 + 2 * FC * n + (h + 1) * FC)
                pe.wait_ge(s["dn_free"], GT * n + i + 1)
                for f in range(FC):
                    last = three_passes(pe, dn[i % 2][:, 0:C], (hT_hi[:, h, f, r], hT_lo[:, h, f, r]),
                                        (w2_hi[:, u, f, :], w2_lo[:, u, f, :]), f == 0, f == FC - 1)
                last.then_inc(s["dn_made"], 1)

        pe.wait_ge(s["eyes"], 2)
        pe.wait_ge(s["rw_lo_made"], 1)
        groups_and_experts(pe, "groups_pe", begin, expert, lambda g: None)

    @block.vector
    def _(dve):
        def begin(g):
            for i in range(4):
                dve.wait_ge(s["xt_hi"], 4 * g + i + 1)
                c = slice(2 * i * P, 2 * (i + 1) * P)
                dve.tensor_tensor(x2T_lo[:, :, c].rearrange("p m (a u) -> p a m u", a=2),
                                  tr[i % 2][:, :].rearrange("p (a m u) -> p a m u", a=2, m=MC),
                                  f32(x2T_hi[:, :, c]).rearrange("p m (a u) -> p a m u", a=2),
                                  ALU.subtract).then_inc(s["xt_taken"], 1)

        def step(ins, g, number):
            ins.then_inc(s["route_step"], 1)
            dve.wait_ge(s["route_step"], g * STEPS + number)

        grid = lambda ap: ap.rearrange("p (i e) -> p i e", e=E)
        over_experts = lambda ap: ap.unsqueeze(2).broadcast_to([P, GT, E])
        over_tiles = lambda ap: ap.unsqueeze(1).broadcast_to([P, GT, E])

        def weights(g):
            dve.wait_ge(s["logits_made"], g + 1)
            step(dve.tensor_tensor(lg[:, :, :], grid(tr[0][:, 0:GT * E]), over_tiles(rb[:, :]), ALU.add), g, 1)
            step(dve.tensor_reduce(lmax[:, :], lg[:, :, :], AX.X, ALU.max), g, 2)
            dve.tensor_tensor(lg[:, :, :], lg[:, :, :], over_experts(lmax[:, :]), ALU.subtract).then_inc(s["shifted"], 1)
            dve.wait_ge(s["exp_made"], g + 1)
            step(dve.tensor_reduce(lsum[:, :], lg[:, :, :], AX.X, ALU.add), g, 3)
            step(dve.reciprocal(lrec[:, :], lsum[:, :]), g, 4)
            step(dve.tensor_tensor(lg[:, :, :], lg[:, :, :], over_experts(lrec[:, :]), ALU.mult), g, 5)
            dve.tensor_scalar(chosen[:, :, :], lg[:, :, :], SMALLEST, None, ALU.is_ge).then_inc(s["chosen_made"], 1)

        def coefficients(g):
            dve.wait_ge(s["ranks_made"], g + 1)
            step(dve.tensor_tensor(rank[:, :, :], grid(tr[1][:, 0:GT * E]), over_tiles(taken_before[:, :]), ALU.add), g, 6)
            step(dve.tensor_tensor(taken_before[:, :], taken_before[:, :], tr[1][:, GT * E:(GT + 1) * E], ALU.add), g, 7)
            step(dve.tensor_scalar(rank[:, :, :], rank[:, :, :], float(CAP), None, ALU.is_le), g, 8)
            step(dve.tensor_tensor(coef[:, :, :], rank[:, :, :], lg[:, :, :], ALU.mult), g, 9)
            step(dve.tensor_reduce(fewest[:, :], taken_before[:, :], AX.X, ALU.min), g, 10)
            step(dve.tensor_scalar(groups_f[:, :], fewest[:, :], float(CAP), float(GROUPS - 1), ALU.is_lt, ALU.mult), g, 11)
            dve.wait_ge(s["w_lo_made"], 2 * E * g + 1)
            dve.tensor_scalar(groups_i[:, :], groups_f[:, :], 1.0, None, ALU.add).then_inc(s["route_step"], 1)

        def expert(g, n, e, u):
            for h in range(2):
                for i in range(FC):
                    dve.wait_ge(s["up_hi"], 2 * FC * n + h * FC + i + 1)
                    dve.scalar_tensor_tensor(hT_lo[:, h, i, :], up[i % 4][:, :], 0.0, f32(hT_hi[:, h, i, :]),
                                             ALU.max, ALU.subtract).then_inc(s["up_free"], 1)
                    if is_first(e) and (h, i) == (1, 1):
                        weights(g)
                if is_first(e) and h == 1:
                    coefficients(g)
            for i in range(GT):
                dve.wait_ge(s["dn_made"], GT * n + i + 1)
                col = coef[:, i, e:e + 1] if isinstance(e, int) else coef[:, i, bass.ds(e, 1)]
                dve.scalar_tensor_tensor(acc[:, i, :], dn[i % 2][:, 0:C], col, acc[:, i, :],
                                         ALU.mult, ALU.add).then_inc(s["dn_free"], 1)
                if isinstance(e, int) and e == E - 1:
                    dve.wait_ge(s["dn_free"], GT * n + i + 1 + 2)
                    dve.bn_stats(bst[:, i, :], acc[:, i, :]).then_inc(s["bst_made"], 1)
                    counted["bst"].wait_next(GT * g + i + 1)
                    dve.bn_aggr(mv[:, i, :], bst[:, i, :]).then_inc(s["mv_made"], 1)

        def end(g):
            pass

        dve.memset(taken_before[:, :], 0.0).then_inc(s["up_free"], 4)
        dve.memset(ones[:, :], 1.0).then_inc(s["dn_free"], 2)
        dve.wait_ge(s["rw_hi_made"], 1)
        dve.wait_ge(s["dn_free"], 2)
        dve.tensor_tensor(rw_lo[:, :, :], rw[:, :, :], f32(rw_hi[:, :, :]), ALU.subtract).then_inc(s["rw_lo_made"], 1)
        counted["bst"] = Counted(dve, s["bst_made"], "count_bst")
        counted["bst"].enter_loop()
        groups_and_experts(dve, "groups_dve", begin, expert, end)


_INS = ["x", "ctx_1024", "mask_BxS2_bf1", "L0_attn_Wq", "L0_attn_bq", "L0_attn_Wk", "L0_attn_bk",
        "L0_attn_Wv", "L0_attn_bv", "L0_attn_Wo", "L0_attn_bo", "L0_attn_ln_g", "L0_attn_ln_b",
        "L0_xattn_Wq", "L0_xattn_Wkv", "L0_xattn_Wout", "L0_xattn_b_out",
        "L0_ffn_router_w", "L0_ffn_router_b", "L0_ffn_experts_inter", "L0_ffn_experts_out"]


def kernel(**inputs):
    import numpy as np
    import concourse.bacc as bacc
    from concourse.bass_utils import run_bass_kernel_spmd

    nc = bacc.Bacc("TRN2", target_bir_lowering=False, num_devices=1)
    arrays, aps = {}, {}
    for name in _INS:
        a = np.ascontiguousarray(inputs[name])
        arrays[f"in_{name}"] = a
        aps[name] = nc.dram_tensor(f"in_{name}", a.shape, mybir.dt.from_np(a.dtype), kind="ExternalInput").ap()
    shape = arrays["in_x"].shape
    aps["out"] = nc.dram_tensor("out_x", shape, F32, kind="ExternalOutput").ap()
    build(nc, aps)
    r = run_bass_kernel_spmd(nc, [arrays], core_ids=[0])
    return r.results[0]["out_x"]
```
